# Optimizing a Trainium2 kernel written in Bass

```python
import numpy as np
import jax
import jax.numpy as jnp

def _softmax(x, axis=-1):
    return jax.nn.softmax(x, axis=axis)

def _gelu(x):
    return jax.nn.gelu(x, approximate=True)

def _silu(x):
    return jax.nn.silu(x)

def _sigmoid(x):
    return jax.nn.sigmoid(x)

def _layernorm(x, axis=-1, eps=1e-05):
    m = jnp.mean(x, axis=axis, keepdims=True)
    v = jnp.var(x, axis=axis, keepdims=True)
    return (x - m) / jnp.sqrt(v + eps)

def _scatter_add(tgt, idx, src, axis=0):
    return tgt.at[idx].add(src)

def _segment_sum(src, seg, n):
    return jax.ops.segment_sum(src, seg, n)
kernel_name = 'mk_xattn_seq_d1_seqx_r4_8f152c'

def setup_inputs(seed: int=0):
    np.random.seed(seed)
    _w = jnp.asarray

    def _rec_inputs():
        import jax
        import jax.numpy as jnp
        _rk = jax.random.key(seed)
        x = -0.0005207 + 1.001 * jax.random.normal(jax.random.fold_in(_rk, 1), (8, 512, 256), jnp.float32)
        _lenS = 512 - jax.random.randint(jax.random.fold_in(_rk, 7), (8,), 0, max(1, 512 // 4) + 1, jnp.int32)
        _lenS2 = 512 - jax.random.randint(jax.random.fold_in(_rk, 8), (8,), 0, max(1, 512 // 4) + 1, jnp.int32)
        _ctx_1024P = jax.random.normal(jax.random.fold_in(_rk, 11), (8, 16, 256), jnp.float32)
        _ctx_1024c = jax.random.dirichlet(jax.random.fold_in(_rk, 511), 0.3 * jnp.ones((16,), jnp.float32), (8, 512))
        _ctx_1024t = jnp.einsum('bsk,bkd->bsd', _ctx_1024c, _ctx_1024P)
        _ctx_1024t = _ctx_1024t * jax.lax.rsqrt(jnp.mean(jnp.square(_ctx_1024t)) + 1e-12) * 0.953939
        ctx_1024 = -0.000514642 + 1.00011 * (_ctx_1024t + 0.3 * jax.random.normal(jax.random.fold_in(_rk, 611), (8, 512, 256), jnp.float32))
        return (x, ctx_1024)
    x, ctx_1024 = _rec_inputs()

    def _L0_xattn_setup():
        import jax, jax.numpy as jnp
        import numpy as np
        B, S, SE, H, NH = (1, 512, 512, 256, 16)
        HD = H // NH
        INNER = 4 * H
        EPS = 1e-05

        def layer_norm(x, g, b):
            mu = jnp.mean(x, axis=-1, keepdims=True)
            var = jnp.mean(jnp.square(x - mu), axis=-1, keepdims=True)
            return (x - mu) * jax.lax.rsqrt(var + EPS) * g + b

        def split_heads(x):
            b, t, _ = x.shape
            return x.reshape(b, t, NH, HD).transpose(0, 2, 1, 3)

        def merge_heads(x):
            b, nh, t, hd = x.shape
            return x.transpose(0, 2, 1, 3).reshape(b, t, nh * hd)

        def _attn_core(q, k, v, extra_bias=None, causal_bool=False, tril_diag2_additive=False):
            w = jnp.einsum('bhqd,bhkd->bhqk', q, k) / jnp.sqrt(jnp.asarray(HD, q.dtype))
            ql, kl = (q.shape[-2], k.shape[-2])
            neg = jnp.finfo(w.dtype).min
            if causal_bool:
                mask = jnp.tril(jnp.ones((ql, kl), bool))
                w = jnp.where(mask[None, None], w, neg)
            if tril_diag2_additive:
                cm = jnp.tril(jnp.ones((ql, kl), w.dtype), k=2)
                w = w + jnp.where(cm == 0, neg, jnp.zeros((), w.dtype))[None, None]
            if extra_bias is not None:
                w = w + extra_bias[:, None, None, :]
            w = jax.nn.softmax(w, axis=-1)
            return jnp.einsum('bhqk,bhkd->bhqd', w, v)
        key = jax.random.key(seed)
        ks = jax.random.split(key, 16)
        n = lambda k, shp: jax.random.normal(k, shp, jnp.float32) * 0.02
        return {'hidden_states': jax.random.normal(ks[0], (B, S, H), jnp.float32), 'encoder_hidden_states': jax.random.normal(ks[1], (B, SE, H), jnp.float32), 'scorer_logits': jax.random.normal(ks[2], (B, SE), jnp.float32), 'ln1_g': jnp.ones((H,), jnp.float32), 'ln1_b': jnp.zeros((H,), jnp.float32), 'c_attn_w': n(ks[3], (H, 3 * H)), 'c_attn_b': jnp.zeros((3 * H,), jnp.float32), 'attn_proj_w': n(ks[4], (H, H)), 'attn_proj_b': jnp.zeros((H,), jnp.float32), 'lnx_g': jnp.ones((H,), jnp.float32), 'lnx_b': jnp.zeros((H,), jnp.float32), 'q_attn_w': n(ks[5], (H, H)), 'q_attn_b': jnp.zeros((H,), jnp.float32), 'x_kv_w': n(ks[6], (H, 2 * H)), 'x_kv_b': jnp.zeros((2 * H,), jnp.float32), 'x_proj_w': n(ks[7], (H, H)), 'x_proj_b': jnp.zeros((H,), jnp.float32), 'ln2_g': jnp.ones((H,), jnp.float32), 'ln2_b': jnp.zeros((H,), jnp.float32), 'fc_w': n(ks[8], (H, INNER)), 'fc_b': jnp.zeros((INNER,), jnp.float32), 'mlp_proj_w': n(ks[9], (INNER, H)), 'mlp_proj_b': jnp.zeros((H,), jnp.float32)}
    _L0_xattn_all = _L0_xattn_setup()
    _L0_xattn_in = {k: v for k, v in _L0_xattn_all.items() if k in ('scorer_logits', 'ln1_g', 'ln1_b', 'c_attn_w', 'c_attn_b', 'attn_proj_w', 'attn_proj_b', 'lnx_g', 'lnx_b', 'q_attn_w', 'q_attn_b', 'x_kv_w', 'x_kv_b', 'x_proj_w', 'x_proj_b', 'ln2_g', 'ln2_b', 'fc_w', 'fc_b', 'mlp_proj_w', 'mlp_proj_b')}
    del _L0_xattn_all
    return {'x': x, 'ctx_1024': ctx_1024, 'L0_xattn_scorer_logits': _L0_xattn_in['scorer_logits'], 'L0_xattn_ln1_g': _L0_xattn_in['ln1_g'], 'L0_xattn_ln1_b': _L0_xattn_in['ln1_b'], 'L0_xattn_c_attn_w': _L0_xattn_in['c_attn_w'], 'L0_xattn_c_attn_b': _L0_xattn_in['c_attn_b'], 'L0_xattn_attn_proj_w': _L0_xattn_in['attn_proj_w'], 'L0_xattn_attn_proj_b': _L0_xattn_in['attn_proj_b'], 'L0_xattn_lnx_g': _L0_xattn_in['lnx_g'], 'L0_xattn_lnx_b': _L0_xattn_in['lnx_b'], 'L0_xattn_q_attn_w': _L0_xattn_in['q_attn_w'], 'L0_xattn_q_attn_b': _L0_xattn_in['q_attn_b'], 'L0_xattn_x_kv_w': _L0_xattn_in['x_kv_w'], 'L0_xattn_x_kv_b': _L0_xattn_in['x_kv_b'], 'L0_xattn_x_proj_w': _L0_xattn_in['x_proj_w'], 'L0_xattn_x_proj_b': _L0_xattn_in['x_proj_b'], 'L0_xattn_ln2_g': _L0_xattn_in['ln2_g'], 'L0_xattn_ln2_b': _L0_xattn_in['ln2_b'], 'L0_xattn_fc_w': _L0_xattn_in['fc_w'], 'L0_xattn_fc_b': _L0_xattn_in['fc_b'], 'L0_xattn_mlp_proj_w': _L0_xattn_in['mlp_proj_w'], 'L0_xattn_mlp_proj_b': _L0_xattn_in['mlp_proj_b']}

def reference(x, ctx_1024, L0_xattn_scorer_logits, L0_xattn_ln1_g, L0_xattn_ln1_b, L0_xattn_c_attn_w, L0_xattn_c_attn_b, L0_xattn_attn_proj_w, L0_xattn_attn_proj_b, L0_xattn_lnx_g, L0_xattn_lnx_b, L0_xattn_q_attn_w, L0_xattn_q_attn_b, L0_xattn_x_kv_w, L0_xattn_x_kv_b, L0_xattn_x_proj_w, L0_xattn_x_proj_b, L0_xattn_ln2_g, L0_xattn_ln2_b, L0_xattn_fc_w, L0_xattn_fc_b, L0_xattn_mlp_proj_w, L0_xattn_mlp_proj_b):
    import jax
    import jax.numpy as jnp

    def _L0_xattn_ref(hidden_states, encoder_hidden_states, scorer_logits, ln1_g, ln1_b, c_attn_w, c_attn_b, attn_proj_w, attn_proj_b, lnx_g, lnx_b, q_attn_w, q_attn_b, x_kv_w, x_kv_b, x_proj_w, x_proj_b, ln2_g, ln2_b, fc_w, fc_b, mlp_proj_w, mlp_proj_b):
        import jax, jax.numpy as jnp
        import numpy as np
        B, S, SE, H, NH = (1, 512, 512, 256, 16)
        HD = H // NH
        INNER = 4 * H
        EPS = 1e-05

        def layer_norm(x, g, b):
            mu = jnp.mean(x, axis=-1, keepdims=True)
            var = jnp.mean(jnp.square(x - mu), axis=-1, keepdims=True)
            return (x - mu) * jax.lax.rsqrt(var + EPS) * g + b

        def split_heads(x):
            b, t, _ = x.shape
            return x.reshape(b, t, NH, HD).transpose(0, 2, 1, 3)

        def merge_heads(x):
            b, nh, t, hd = x.shape
            return x.transpose(0, 2, 1, 3).reshape(b, t, nh * hd)

        def _attn_core(q, k, v, extra_bias=None, causal_bool=False, tril_diag2_additive=False):
            w = jnp.einsum('bhqd,bhkd->bhqk', q, k) / jnp.sqrt(jnp.asarray(HD, q.dtype))
            ql, kl = (q.shape[-2], k.shape[-2])
            neg = jnp.finfo(w.dtype).min
            if causal_bool:
                mask = jnp.tril(jnp.ones((ql, kl), bool))
                w = jnp.where(mask[None, None], w, neg)
            if tril_diag2_additive:
                cm = jnp.tril(jnp.ones((ql, kl), w.dtype), k=2)
                w = w + jnp.where(cm == 0, neg, jnp.zeros((), w.dtype))[None, None]
            if extra_bias is not None:
                w = w + extra_bias[:, None, None, :]
            w = jax.nn.softmax(w, axis=-1)
            return jnp.einsum('bhqk,bhkd->bhqd', w, v)
        residual = hidden_states
        x = layer_norm(hidden_states, ln1_g, ln1_b)
        qkv = x @ c_attn_w + c_attn_b
        q, k, v = jnp.split(qkv, 3, axis=-1)
        a = _attn_core(split_heads(q), split_heads(k), split_heads(v), causal_bool=True)
        a = merge_heads(a) @ attn_proj_w + attn_proj_b
        hidden_states = a + residual
        residual = hidden_states
        x = layer_norm(hidden_states, lnx_g, lnx_b)
        q = x @ q_attn_w + q_attn_b
        kv = encoder_hidden_states @ x_kv_w + x_kv_b
        k, v = jnp.split(kv, 2, axis=-1)
        a = _attn_core(split_heads(q), split_heads(k), split_heads(v), extra_bias=scorer_logits, tril_diag2_additive=True)
        a = merge_heads(a) @ x_proj_w + x_proj_b
        hidden_states = residual + a
        residual = hidden_states
        x = layer_norm(hidden_states, ln2_g, ln2_b)
        h = jax.nn.gelu(x @ fc_w + fc_b, approximate=True)
        hidden_states = residual + (h @ mlp_proj_w + mlp_proj_b)
        return hidden_states
    x = _L0_xattn_ref(x, ctx_1024, L0_xattn_scorer_logits, L0_xattn_ln1_g, L0_xattn_ln1_b, L0_xattn_c_attn_w, L0_xattn_c_attn_b, L0_xattn_attn_proj_w, L0_xattn_attn_proj_b, L0_xattn_lnx_g, L0_xattn_lnx_b, L0_xattn_q_attn_w, L0_xattn_q_attn_b, L0_xattn_x_kv_w, L0_xattn_x_kv_b, L0_xattn_x_proj_w, L0_xattn_x_proj_b, L0_xattn_ln2_g, L0_xattn_ln2_b, L0_xattn_fc_w, L0_xattn_fc_b, L0_xattn_mlp_proj_w, L0_xattn_mlp_proj_b)
    return x

_drawn_inputs = setup_inputs


def setup_inputs(seed=0):
    import zlib

    import numpy as np

    out = dict(_drawn_inputs(seed))
    spreads = {'L0_xattn_ln1_g': (1.0, 0.6),
     'L0_xattn_ln1_b': (0.0, 0.723),
     'L0_xattn_c_attn_b': (0.0, 0.269),
     'L0_xattn_attn_proj_b': (0.0, 0.1),
     'L0_xattn_lnx_g': (1.0, 0.6),
     'L0_xattn_lnx_b': (0.0, 2.0),
     'L0_xattn_q_attn_b': (0.0, 2.0),
     'L0_xattn_x_kv_b': (0.0, 0.272),
     'L0_xattn_x_proj_b': (0.0, 0.1),
     'L0_xattn_ln2_g': (1.0, 0.6),
     'L0_xattn_ln2_b': (0.0, 0.638),
     'L0_xattn_fc_b': (0.0, 0.1),
     'L0_xattn_mlp_proj_b': (0.0, 0.1)}
    factors = {'L0_xattn_scorer_logits': 5.888, 'L0_xattn_c_attn_w': 3.473, 'L0_xattn_q_attn_w': 8.0}
    for name, (base, spread) in spreads.items():
        noise = np.random.default_rng([zlib.crc32(name.encode()), seed]).standard_normal(out[name].shape)
        drawn = base * np.exp(spread * noise) if base else spread * noise
        out[name] = jnp.asarray(drawn.astype(out[name].dtype))
    for name, factor in factors.items():
        out[name] = (out[name] * factor).astype(out[name].dtype)
    return out
```

```python
from contextlib import ExitStack

import numpy as np

import concourse.bass as bass
from concourse import mybir

F32 = mybir.dt.float32
BF16 = mybir.dt.bfloat16
ACT = mybir.ActivationFunctionType
ALU = mybir.AluOpType
AX = mybir.AxisListType

P = 128
NB, T, H = 8, 512, 256
NH = 16
HD = H // NH
INNER = 4 * H
EPS = 1e-5
SCALE = HD ** -0.5
TB = T // P
HC = H // P
FC = INNER // P
GH = 4
NG = NH // GH
HP = NH // HC
VW = HD + 1
VROW = NH * VW + (32 - VW)
NEG = -3.0e38
STACK = 6 * HD
LAST = {"self": 0, "cross": 2}
KMAX = {"self": STACK, "cross": STACK + 3}
KALL = {kind: KMAX[kind] + 2 for kind in KMAX}
PARTS = {"q": (0, 1, 0, 1, 2, 0), "k": (0, 0, 1, 1, 0, 2)}

COLS = {}
for _name, _n in (("ln1_g", HC), ("ln1_b", HC), ("lnx_g", HC), ("lnx_b", HC), ("ln2_g", HC),
                  ("ln2_b", HC), ("q1", HC), ("k1", HC), ("q2", HC), ("k2", HC), ("fc_b", FC)):
    COLS[_name] = (sum(n for _, n in COLS.values()), _n)
NCOL = sum(n for _, n in COLS.values())
ROWS = ("v1", "proj1", "v2", "proj2", "mlp")

PLAN = {
    "X": (
        "R2 M0 S0 R1 PV tc.0 tc.1 M1 S1 k2.0 k2.1 M2 S2 ta1.0 ta1.1 M3 p1.0 p1.1 ON MT S3",
        "M0 S0 PV M1 S1 tx.0 tx.1 M2 S2 q2.0 M3 q2.1 ON MT S3",
        "M0 S0 PV v2.0 M1 S1 M2 S2 M3 v2.1 ON MT S3",
        "M0 S0 PV L1 M1 S1 M2 S2 M3 ON MT S3",
    ),
    "Y": (
        "M0 S0 PV t1.0 t1.1 M1 S1 ta2.0 ta2.1 M2 S2 q1.0 q1.1 M3 p2.0 p2.1 ON MT S3",
        "M0 S0 PV k1.0 k1.1 M1 S1 t2.0 t2.1 M2 S2 v1.0 M3 v1.1 ON MT S3",
        "M0 S0 PV f.0 f.1 f.2 f.3 M1 S1 M2 S2 M3 f.4 f.5 f.6 f.7 ON MT S3",
        "M0 S0 PV m.0 M1 S1 m.1 M2 S2 m.2 M3 m.3 ON MT S3",
    ),
}
OFFSET = {"L1": 1, "t1": 1, "q1": 1, "k1": 1, "v1": 1,
          "tc": -1, "k2": -1, "v2": -1, "ta1": -1, "R1": -1, "p1": -1, "tx": -1, "q2": -1,
          "R2": -2, "ta2": -2, "p2": -2, "t2": -2, "f": -2, "m": -2}
ATTENTION = ("M", "S", "PV", "ON", "MT")
FIRST, LOOP_FROM, LOOP_TO, END = -1, 3, NB - 1, NB + 2


class Attn:

    def __init__(self, kind, like, i):
        off = 0 if kind == "self" else -1
        self.kind, self.like, self.b = kind, like + off, i + off
        if kind == "self":
            self.n = 0 if self.like == 0 else 2 * self.b - 1
        else:
            self.n = 2 * NB - 1 if self.like == NB - 1 else 2 * self.b + 2


def attention_of(slot, like, i):
    if slot == "X":
        return Attn("self", like, i) if 0 <= like < NB else None
    return Attn("cross", like, i) if 1 <= like <= NB else None


def items(like, i):
    slots = [("Y", like - 1, i - 1), ("X", like, i), ("Y", like, i), ("X", like + 1, i + 1)]
    around = [attention_of(*s) for s in slots]
    for s, slot in ((1, "X"), (2, "Y")):
        before, now, after = around[s - 1:s + 2]
        for step, text in enumerate(PLAN[slot]):
            for word in text.split():
                name, _, part = word.partition(".")
                part = int(part) if part else 0
                if word[0] in "MS" and word[1:].isdigit():
                    name, part = word[0], int(word[1:])
                if name in ("M", "MT"):
                    at, g = (now, step + 1) if step < NG - 1 else (after, 0)
                elif name == "S":
                    at, g = now, step
                elif name in ("PV", "ON"):
                    at, g = (now, step - 1) if step else (before, NG - 1)
                else:
                    b = like + OFFSET[name]
                    if 0 <= b < NB:
                        yield name, part, b, i + OFFSET[name], None, None
                    continue
                if at is not None:
                    yield name, part, at.like, at.b, at, g


def is_dense(name):
    return name not in ("M", "S", "PV", "R1", "R2", "L1")


def dense_count(like):
    return sum(is_dense(item[0]) for item in items(like, like))


PER_LOOP = dense_count(LOOP_FROM)
assert PER_LOOP % 2 == 0
BEFORE = {}
_n = 0
for _like in range(FIRST, END):
    BEFORE[_like] = _n
    _n += dense_count(_like)


def widths(kind):
    return [min(T, P * (q + 1) + LAST[kind]) for q in range(TB)]


def block_kernel(nc, x, ctx, logits, w_qkv, w_proj1, w_q2, w_kv2, w_proj2, w_fc, w_mlp, cols, rows, out):
    with ExitStack() as stack:
        def sb(name, shape, dt=F32):
            return stack.enter_context(nc.sbuf_tensor(name, shape, dt))

        def sem(name):
            return stack.enter_context(nc.semaphore(name))

        max_scores = stack.enter_context(nc.psum_tensor("max_scores", [P, 2, T], F32))
        scores = stack.enter_context(nc.psum_tensor("scores", [P, 3, T], F32))
        pv_out = stack.enter_context(nc.psum_tensor("pv_out", [P, T], F32))
        dense = stack.enter_context(nc.psum_tensor("dense", [P, 2, T], F32))

        qkv_w = sb("qkv_w", [P, HC, 3 * H])
        proj1_w = sb("proj1_w", [P, HC, H])
        q2_w = sb("q2_w", [P, HC, H])
        kv2_w = sb("kv2_w", [P, HC, 2 * H])
        proj2_w = sb("proj2_w", [P, HC, H])
        fc_w = sb("fc_w", [P, HC, INNER])
        mlp_w = sb("mlp_w", [P, FC, H])
        col = sb("col", [P, NCOL])
        row = sb("row", [P, len(ROWS), H])
        ident = sb("ident", [P, P])
        ident_b = sb("ident_b", [P, P], BF16)
        mask = {"self": sb("mask_self", [P, P], BF16), "cross": sb("mask_cross", [P, P + 2], BF16)}
        minus_half = sb("minus_half", [P, TB])

        x_in = sb("x_in", [P, TB, H])
        hidden1 = sb("hidden1", [P, TB, H])
        hidden2 = sb("hidden2", [P, TB, H])
        normed = sb("normed", [P, TB, H])
        attn_out = {"self": sb("attn1", [P, TB, H]), "cross": sb("attn2", [P, TB, H])}
        feat_a = sb("feat_a", [P, HC, T])
        feat_b = sb("feat_b", [P, HC, T])
        inner = sb("inner", [P, FC, T])
        key_bias = inner[0:1, 0, :]
        key_rest = inner[0:1, 1:3, :]
        key_parts = inner[0:1, 3:5, :].bitcast(BF16).rearrange("p a (b t) -> p (a b) t", t=T)
        parts = {s: sb(f"parts_{s}", [P, 3, HC, T], BF16) for s in "qk"}
        rest = sb("rest", [P, HC, T])
        q_stack = {k: sb(f"q_stack_{k}", [KALL[k], NH, T], BF16) for k in KALL}
        k_stack = {k: sb(f"k_stack_{k}", [KALL[k], NH, T], BF16) for k in KALL}
        v_ones = {k: sb(f"v_ones_{k}", [P, TB, VROW]) for k in KALL}
        row_max = sb("row_max", [P, 2, GH * TB])
        max_parts = sb("max_parts", [P, P], BF16)
        max_rows = sb("max_rows", [2 * GH * TB, P], BF16)
        WMAX = sum(widths("cross"))
        probs = sb("probs", [P, 2 * GH, WMAX])
        o_turn = sb("o_turn", [P, T])
        recip = sb("recip", [P, 2, TB, GH])
        stats = sb("stats", [P, TB, 6])
        mean_var = sb("mean_var", [P, TB, 2])
        var_eps = sb("var_eps", [P, TB])
        rstd = sb("rstd", [P, TB])
        mean_rstd = sb("mean_rstd", [P, TB])
        shift = sb("shift", [P, TB])

        weights_loaded = sem("weights_loaded")
        params_loaded = sem("params_loaded")
        consts_pool = sem("consts_pool")
        consts_dve = sem("consts_dve")
        bias_rows_loaded = sem("bias_rows_loaded")
        x_loaded = sem("x_loaded")
        ctx_loaded = sem("ctx_loaded")
        resid_loaded = sem("resid_loaded")
        out_stored = sem("out_stored")
        stack_loaded = {n: sem(f"{n}_stacked") for n in ("q1", "k1", "q2", "k2")}
        max_loaded = sem("max_loaded")
        dense_made = sem("dense_made")
        max_scores_made = sem("max_scores_made")
        max_scores_read = sem("max_scores_read")
        scores_made = sem("scores_made")
        exp_done = sem("exp_done")
        masked = sem("masked")
        pv_done = sem("pv_done")
        o_copied = sem("o_copied")
        max_hi = sem("max_hi")
        max_split = sem("max_split")
        max_rows_ready = sem("max_rows_ready")
        recip_ready = sem("recip_ready")
        attn_ready = sem("attn_ready")
        turned = {n: sem(f"{n}_turned") for n in ("t1", "tc", "tx", "t2", "ta1", "ta2")}
        hi = {n: sem(f"{n}_hi") for n in stack_loaded}
        remains = {n: sem(f"{n}_rest") for n in stack_loaded}
        mid = {n: sem(f"{n}_mid") for n in stack_loaded}
        lo = {n: sem(f"{n}_lo") for n in stack_loaded}
        v_ready = {n: sem(f"{n}_ready") for n in ("v1", "v2")}
        sum_ready = {n: sem(f"{n}_sum") for n in ("p1", "p2")}
        gelu_ready = sem("gelu_ready")
        out_ready = sem("out_ready")
        resid_ready = {n: sem(f"{n}_added") for n in ("R1", "R2", "R3")}
        stats_ready = {n: sem(f"stats_{n}") for n in ("t1", "tx", "t2")}
        aggr_ready = {n: sem(f"aggr_{n}") for n in ("t1", "tx", "t2")}
        norm_step = {n: sem(f"norm_step_{n}") for n in ("t1", "tx", "t2")}
        norm_ready = {n: sem(f"norm_{n}") for n in ("t1", "tx", "t2")}

        gates_passed = sem("gates_passed")

        block = stack.enter_context(nc.Block())

        def dense_of(like, i):
            if LOOP_FROM <= like < LOOP_TO:
                return BEFORE[LOOP_FROM] + (i - LOOP_FROM) * PER_LOOP
            return BEFORE[like]

        def wait(eng, sem_, value):
            if not (isinstance(value, int) and value <= 0):
                eng.wait_ge(sem_, value)

        def gate(eng, sem_, value):
            eng.wait_ge(sem_, value)
            eng.sem_inc(gates_passed, 1)

        def iterations(eng, body):
            for like in range(FIRST, LOOP_FROM):
                body(like, like)
            with eng.Fori(LOOP_FROM, LOOP_TO) as i:
                body(LOOP_FROM, i)
            for like in range(LOOP_TO, END):
                body(like, like)

        def released(item):
            name, part, _, b, at, g = item
            if name == "MT":
                return max_rows_ready, at.n * NG + g + 1
            if name == "ON":
                return attn_ready, at.n * NG + g + 1
            if name in turned:
                return turned[name], b * HC + part + 1
            if name in remains:
                return remains[name], b * HC + part + 1
            if name in v_ready:
                return v_ready[name], b * 2 + part + 1
            if name in sum_ready:
                return sum_ready[name], b * 2 + part + 1
            if name == "f":
                return gelu_ready, b * FC + part + 1
            return out_ready, b * TB + part + 1

        def mask_of(kind, q):
            return mask[kind][:, 0:widths(kind)[q] - P * q]

        def prob_cols(kind):
            at, found = 0, []
            for k in range(TB):
                w = widths(kind)[TB - 1 - k]
                found.append((at, T - w, w))
                at += w
            return found

        @block.sync
        def _(sp):
            sp.dma_start(x_in[:], x[0].rearrange("(t p) h -> p t h", p=P)).then_inc(x_loaded, 16)
            sp.dma_start(col[:], cols).then_inc(params_loaded, 16)
            sp.dma_start(qkv_w[:], w_qkv.rearrange("(c p) n -> p c n", p=P)).then_inc(weights_loaded, 16)
            sp.dma_start(row[:], rows.partition_broadcast(P)).then_inc(params_loaded, 16)
            sp.dma_start(key_bias[:], logits).then_inc(params_loaded, 16)
            for dst, src in ((proj1_w, w_proj1), (kv2_w, w_kv2), (q2_w, w_q2), (proj2_w, w_proj2),
                             (fc_w, w_fc), (mlp_w, w_mlp)):
                sp.dma_start(dst[:], src.rearrange("(c p) n -> p c n", p=P)).then_inc(weights_loaded, 16)
            sp.wait_ge(consts_dve, DVE_CONSTS)
            for r in range(3):
                sp.dma_start(k_stack["cross"][STACK + r:STACK + r + 1, :, :],
                             key_parts[0:1, r:r + 1, :].to_broadcast([1, NH, T])).then_inc(bias_rows_loaded, 16)

            def body(like, i):
                for name, part, blike, b, at, g in items(like, i):
                    if name == "R1":
                        wait(sp, resid_ready["R2"], b)
                        sp.dma_start(hidden1[:], x[b].rearrange("(t p) h -> p t h", p=P)).then_inc(resid_loaded, 16)
                    if name == "tc" and part == HC - 1 and blike + 2 < NB:
                        wait(sp, turned["tc"], (b + 1) * HC)
                        sp.dma_start(x_in[:], x[b + 2].rearrange("(t p) h -> p t h", p=P)).then_inc(x_loaded, 16)
                    if name == "t1" and part == HC - 1 and blike > 0:
                        wait(sp, turned["t1"], (b + 1) * HC)
                        sp.dma_start(x_in[:], ctx[b - 1].rearrange("(t p) h -> p t h", p=P)).then_inc(ctx_loaded, 16)
                    if name in stack_loaded and part == HC - 1:
                        kind = "self" if name[1] == "1" else "cross"
                        dst = (q_stack if name[0] == "q" else k_stack)[kind]
                        if blike > 0:
                            before = Attn(kind, blike - 1 + (kind == "cross"), b - 1 + (kind == "cross"))
                            wait(sp, scores_made, (before.n + 1) * NH * 3)
                        src = parts[name[0]]
                        for p_, ready in ((0, hi), (1, mid), (2, lo)):
                            sp.wait_ge(ready[name], (b + 1) * HC)
                            for r, which in enumerate(PARTS[name[0]]):
                                if which == p_:
                                    sp.dma_start(dst[r * HD:(r + 1) * HD, :, :],
                                                 src[:, p_].rearrange("p c t -> p (c t)")).then_inc(stack_loaded[name], 16)
                    if name == "MT":
                        sp.wait_ge(max_rows_ready, at.n * NG + g + 1)
                        sp.dma_start(q_stack[at.kind][KMAX[at.kind]:KALL[at.kind], g * GH:(g + 1) * GH, :],
                                     max_rows[:]).then_inc(max_loaded, 16)
                    if name == "m":
                        sp.wait_ge(out_ready, b * TB + part + 1)
                        sp.dma_start(out[b, part * P:(part + 1) * P, :], hidden2[:, part, :]).then_inc(out_stored, 16)
                if like == NB - 1:
                    sp.wait_ge(turned["tc"], (NB - 1) * HC)
                    sp.dma_start(x_in[:], ctx[NB - 1].rearrange("(t p) h -> p t h", p=P)).then_inc(ctx_loaded, 16)

            body(FIRST, FIRST)
            sp.wait_ge(turned["t1"], HC)
            sp.dma_start(x_in[:], x[1].rearrange("(t p) h -> p t h", p=P)).then_inc(x_loaded, 16)
            for like in range(FIRST + 1, LOOP_FROM):
                body(like, like)
            with sp.Fori(LOOP_FROM, LOOP_TO) as i:
                body(LOOP_FROM, i)
            for like in range(LOOP_TO, END):
                body(like, like)
            sp.wait_ge(out_stored, NB * TB * 16)

        @block.tensor
        def _(pe):
            pe.wait_ge(weights_loaded, 16)
            pe.wait_ge(consts_pool, POOL_CONSTS)
            pe.wait_ge(consts_dve, DVE_CONSTS)

            def turn(dst, src, part):
                for t in range(TB):
                    last = pe.transpose(dst[:, t * P:(t + 1) * P], src[:, t, part * P:(part + 1) * P], ident[:])
                return last

            def by_feature(dst, w, at, src):
                for c in range(HC):
                    last = pe.matmul(dst, w[:, c, at:at + P], src[:, c, :], start=(c == 0), stop=(c == HC - 1))
                return last

            def by_token(dst, src, w, at, t, chunks=HC):
                for c in range(chunks):
                    last = pe.matmul(dst, src[:, c, t * P:(t + 1) * P], w[:, c, at:at + H],
                                     start=(c == 0), stop=(c == chunks - 1))
                return last

            def body(like, i):
                k = 0
                for item in items(like, i):
                    name, part, blike, b, at, g = item
                    if name == "M":
                        head = g * GH + part
                        if head == 0:
                            n = "1" if at.kind == "self" else "2"
                            pe.wait_ge(stack_loaded["q" + n], (at.b + 1) * 6 * 16)
                            pe.wait_ge(stack_loaded["k" + n], (at.b + 1) * 6 * 16)
                            if at.kind == "cross" and at.like == 0:
                                pe.wait_ge(bias_rows_loaded, 3 * 16)
                        rows_ = KMAX[at.kind]
                        W = widths(at.kind)
                        for r, blocks in enumerate(((3,), (2,), (1, 0))):
                            tile = at.n * NH * 3 + head * 3 + r
                            bank = (head * 3 + r) % 2
                            wait(pe, max_scores_read, tile - 1)
                            c0 = 0
                            for q in blocks:
                                pe.matmul(max_scores[:, bank, c0:c0 + W[q]],
                                          q_stack[at.kind][0:rows_, head, q * P:(q + 1) * P],
                                          k_stack[at.kind][0:rows_, head, 0:W[q]], start=True, stop=False)
                                m = mask_of(at.kind, q)
                                last = pe.matmul(max_scores[:, bank, c0 + q * P:c0 + W[q]], ident_b[:], m,
                                                 start=False, stop=True)
                                c0 += W[q]
                            last.then_inc(max_scores_made, 1)
                    elif name == "S":
                        head = g * GH + part
                        if part == 0:
                            pe.wait_ge(max_loaded, (at.n * NG + g + 1) * 16)
                        rows_ = KALL[at.kind]
                        cols_ = prob_cols(at.kind)
                        for r, blocks in enumerate(((0,), (1,), (2, 3))):
                            wait(pe, exp_done, at.n * NH * 3 + head * 3 + r - 2)
                            c0 = 0
                            for kb in blocks:
                                _, q0, w = cols_[kb]
                                last = pe.matmul(scores[:, r, c0:c0 + w],
                                                 k_stack[at.kind][0:rows_, head, kb * P:(kb + 1) * P],
                                                 q_stack[at.kind][0:rows_, head, q0:T], start=True, stop=True)
                                c0 += w
                            last.then_inc(scores_made, 1)
                    elif name == "PV":
                        pe.wait_ge(masked, at.n * NH * 2 + (g + 1) * GH * 2)
                        if g == 0:
                            pe.wait_ge(v_ready["v1" if at.kind == "self" else "v2"], (at.b + 1) * 2)
                        for kb, (c0, q0, w) in enumerate(prob_cols(at.kind)):
                            for j in range(GH):
                                head = g * GH + j
                                last = pe.matmul(pv_out[32 * j:32 * j + 32, q0:T],
                                                 v_ones[at.kind][:, kb, head * VW:head * VW + 32],
                                                 probs[:, head % (2 * GH), c0:c0 + w],
                                                 start=(kb == 0), stop=(kb == TB - 1))
                        last.then_inc(pv_done, 1)
                    if not is_dense(name):
                        continue
                    n = BEFORE[like] + k
                    bank = n % 2
                    if k >= 2:
                        wait(pe, *released(recent[-2]))
                    elif n >= 2:
                        earlier = [x_ for x_ in items(like - 1, i - 1) if is_dense(x_[0])]
                        if like - 1 == FIRST:
                            earlier = [x_ for x_ in items(like - 1, like - 1) if is_dense(x_[0])]
                        wait(pe, *released((earlier + recent)[-2] if k else earlier[-2]))
                    if k == 0:
                        recent = []
                    recent.append(item)
                    k += 1
                    d = dense[:, bank, :]
                    if name == "MT":
                        pe.wait_ge(max_split, at.n * NG + g + 1)
                        last = pe.transpose(d.bitcast(BF16)[:, 0:P], max_parts[:], ident_b[:])
                    elif name == "ON":
                        pe.wait_ge(o_copied, at.n * NG + g + 1)
                        for t in range(TB):
                            last = pe.transpose(d[:, t * P:(t + 1) * P], o_turn[:, t * P:(t + 1) * P], ident[:])
                    elif name in ("t1", "tx", "t2"):
                        pe.wait_ge(norm_ready[name], (b + 1) * TB)
                        last = turn(d, x_in if name == "t1" else normed, part)
                    elif name == "tc":
                        pe.wait_ge(ctx_loaded, (b + 1) * 16)
                        last = turn(d, x_in, part)
                    elif name in ("ta1", "ta2"):
                        kind = "self" if name == "ta1" else "cross"
                        a = Attn(kind, blike + (kind == "cross"), b + (kind == "cross"))
                        pe.wait_ge(attn_ready, (a.n + 1) * NG)
                        last = turn(d, attn_out[kind], part)
                    elif name in ("q1", "k1"):
                        pe.wait_ge(turned["t1"], (b + 1) * HC)
                        last = by_feature(d, qkv_w, (name == "k1") * H + part * P, feat_a)
                    elif name == "q2":
                        pe.wait_ge(turned["tx"], (b + 1) * HC)
                        last = by_feature(d, q2_w, part * P, feat_b)
                    elif name == "k2":
                        pe.wait_ge(turned["tc"], (b + 1) * HC)
                        last = by_feature(d, kv2_w, part * P, feat_a)
                    elif name in ("v1", "v2"):
                        pe.wait_ge(turned["t1" if name == "v1" else "tc"], (b + 1) * HC)
                        w, c0 = (qkv_w, 2 * H) if name == "v1" else (kv2_w, H)
                        for t in range(2):
                            last = by_token(d[:, t * H:(t + 1) * H], feat_a, w, c0, 2 * part + t)
                    elif name in ("p1", "p2"):
                        pe.wait_ge(turned["ta1" if name == "p1" else "ta2"], (b + 1) * HC)
                        for t in range(2):
                            last = by_token(d[:, t * H:(t + 1) * H], feat_b,
                                            proj1_w if name == "p1" else proj2_w, 0, 2 * part + t)
                    elif name == "f":
                        pe.wait_ge(turned["t2"], (b + 1) * HC)
                        last = by_feature(d, fc_w, part * P, feat_b)
                    else:
                        pe.wait_ge(gelu_ready, (b + 1) * FC)
                        last = by_token(d[:, 0:H], inner, mlp_w, 0, part, FC)
                    last.then_inc(dense_made, 1)
                if like == FIRST:
                    pe.wait_ge(weights_loaded, 7 * 16)

            iterations(pe, body)

        @block.scalar
        def _(act):
            act.wait_ge(params_loaded, 3 * 16)

            def column(name, part):
                at = COLS[name][0] + part
                return col[:, at:at + 1]

            def body(like, i):
                made = dense_of(like, i)
                for name, part, blike, b, at, g in items(like, i):
                    if is_dense(name):
                        made = made + 1
                        d = dense[:, (BEFORE[like] + is_first[0]) % 2, :]
                        is_first[0] += 1
                    if name == "S":
                        head = g * GH + part
                        if part == 0:
                            wait(act, pv_done, at.n * NG + g - 1)
                        cols_ = prob_cols(at.kind)
                        for r, (c0, w) in enumerate(((cols_[0][0], cols_[0][2]), (cols_[1][0], cols_[1][2]),
                                                     (cols_[2][0], cols_[2][2] + cols_[3][2]))):
                            act.wait_ge(scores_made, at.n * NH * 3 + head * 3 + r + 1)
                            nc.scalar.activation(probs[:, head % (2 * GH), c0:c0 + w], scores[:, r, 0:w],
                                                 ACT.Exp, scale=SCALE).then_inc(exp_done, 1)
                    elif name == "PV":
                        act.wait_ge(pv_done, at.n * NG + g + 1)
                        nc.scalar.copy(o_turn[:], pv_out[:]).then_inc(o_copied, 1)
                    elif name in ("t1", "tx", "t2"):
                        ln = {"t1": "ln1", "tx": "lnx", "t2": "ln2"}[name]
                        act.wait_ge(dense_made, made)
                        nc.scalar.activation((feat_a if name == "t1" else feat_b)[:, part, :], d, ACT.Identity,
                                             bias=column(ln + "_b", part), scale=column(ln + "_g", part)
                                             ).then_inc(turned[name], 1)
                    elif name in ("tc", "ta1", "ta2"):
                        act.wait_ge(dense_made, made)
                        nc.scalar.copy((feat_a if name == "tc" else feat_b)[:, part, :], d).then_inc(turned[name], 1)
                    elif name in hi:
                        if part == 0:
                            if name[1] == "1":
                                wait(act, stack_loaded[name[0] + "2"], (b - 1) * 96 if blike >= 2 else 0)
                            else:
                                wait(act, stack_loaded[name[0] + "1"], (b + 2) * 96 if blike + 2 <= NB else NB * 96)
                        act.wait_ge(dense_made, made)
                        nc.scalar.activation(parts[name[0]][:, 0, part, :], d, ACT.Identity,
                                             bias=column(name, part)).then_inc(hi[name], 1)
                    elif name == "f":
                        act.wait_ge(dense_made, made)
                        nc.scalar.activation(inner[:, part, :], d, ACT.Gelu_apprx_tanh,
                                             bias=column("fc_b", part)).then_inc(gelu_ready, 1)

            is_first = [0]

            def counted(like, i):
                is_first[0] = 0
                body(like, i)

            iterations(act, counted)

        @block.vector
        def _(dve):
            for kind in KALL:
                nc.vector.memset(v_ones[kind][:], 1.0)
            nc.vector.memset(k_stack["self"][STACK:KALL["self"], :, :], -1.0)
            nc.vector.memset(k_stack["cross"][STACK:KALL["cross"], :, :], -1.0)
            nc.vector.memset(q_stack["cross"][STACK:KALL["cross"], :, :], 1.0)
            nc.vector.memset(max_parts[:], 0.0)
            nc.vector.memset(minus_half[:], -0.5)
            dve.wait_ge(consts_pool, POOL_CONSTS)
            nc.vector.tensor_copy(ident_b[:], ident[:]).then_inc(consts_dve, 1)
            dve.wait_ge(params_loaded, 3 * 16)
            steps = (
                lambda: nc.vector.tensor_scalar_mul(key_bias[:], key_bias[:], 1.0 / SCALE),
                lambda: nc.vector.tensor_copy(key_parts[:, 0, :], key_bias[:]),
                lambda: nc.vector.tensor_tensor(key_rest[:, 0, :], key_bias[:], key_parts[:, 0, :], ALU.subtract),
                lambda: nc.vector.tensor_copy(key_parts[:, 1, :], key_rest[:, 0, :]),
                lambda: nc.vector.tensor_tensor(key_rest[:, 1, :], key_rest[:, 0, :], key_parts[:, 1, :], ALU.subtract),
                lambda: nc.vector.tensor_copy(key_parts[:, 2, :], key_rest[:, 1, :]),
            )
            for n, step in enumerate(steps):
                if n:
                    dve.wait_ge(consts_dve, n + 1)
                step().then_inc(consts_dve, 1)

            def column(name, part):
                at = COLS[name][0] + part
                return col[:, at:at + 1]

            def bias_row(name):
                return row[:, ROWS.index(name), :]

            def statistics(name, src, b):
                for t in range(TB):
                    last = nc.vector.bn_stats(stats[:, t, :], src[:, t, :])
                last.then_inc(stats_ready[name], 1)
                gate(dve, stats_ready[name], b + 1)
                for t in range(TB):
                    last = nc.vector.bn_aggr(mean_var[:, t, :], stats[:, t, :])
                last.then_inc(aggr_ready[name], 1)

            def body(like, i):
                made, k = dense_of(like, i), 0
                for name, part, blike, b, at, g in items(like, i):
                    if is_dense(name):
                        made = made + 1
                        d = dense[:, (BEFORE[like] + k) % 2, :]
                        k += 1
                    if name == "L1":
                        dve.wait_ge(x_loaded, (b + 1) * 16)
                        if blike >= 3:
                            dve.wait_ge(norm_step["t2"], (b - 3) * 4)
                        if blike >= 2:
                            dve.wait_ge(norm_step["tx"], (b - 1) * 4)
                        statistics("t1", x_in, b)
                    elif name == "M":
                        head = g * GH + part
                        W = widths(at.kind)
                        for r, blocks in enumerate(((3,), (2,), (1, 0))):
                            tile = at.n * NH * 3 + head * 3 + r
                            dve.wait_ge(max_scores_made, tile + 1)
                            c0 = 0
                            for q in blocks:
                                c = part * TB + q
                                last = nc.vector.tensor_reduce(row_max[:, g % 2, c:c + 1],
                                                               max_scores[:, (head * 3 + r) % 2, c0:c0 + W[q]],
                                                               AX.X, ALU.max)
                                c0 += W[q]
                            last.then_inc(max_scores_read, 1)
                        if part == GH - 1:
                            n = GH * TB
                            dve.wait_ge(max_scores_read, at.n * NH * 3 + (g + 1) * GH * 3)
                            nc.vector.tensor_copy(max_parts[:, 0:n], row_max[:, g % 2, :]).then_inc(max_hi, 1)
                            dve.wait_ge(max_hi, at.n * NG + g + 1)
                            nc.vector.tensor_tensor(max_parts[:, n:2 * n], row_max[:, g % 2, :], max_parts[:, 0:n],
                                                    ALU.subtract).then_inc(max_split, 1)
                    elif name == "MT":
                        dve.wait_ge(dense_made, made)
                        wait(dve, max_loaded, (at.n * NG + g) * 16)
                        nc.vector.tensor_copy(max_rows[:], d.bitcast(BF16)[0:2 * GH * TB, 0:P]).then_inc(max_rows_ready, 1)
                    elif name == "ON":
                        o = d.rearrange("p (q h e) -> p q h e", q=TB, h=GH)
                        dve.wait_ge(dense_made, made)
                        nc.vector.reciprocal(recip[:, g % 2], o[:, :, :, HD]).then_inc(recip_ready, 1)
                        dve.wait_ge(recip_ready, at.n * NG + g + 1)
                        dst = attn_out[at.kind][:, :, g * GH * HD:(g + 1) * GH * HD]
                        nc.vector.tensor_tensor(dst.rearrange("p q (h e) -> p q h e", h=GH), o[:, :, :, 0:HD],
                                                recip[:, g % 2].unsqueeze(3).to_broadcast([P, TB, GH, HD]),
                                                ALU.mult).then_inc(attn_ready, 1)
                    elif name in hi:
                        n = b * HC + part + 1
                        if name == "k2":
                            wait(dve, lo["k1"], (b + 1) * HC + part + 1 if blike + 1 < NB else NB * HC - HC + part + 1)
                        elif name == "q2":
                            dve.wait_ge(lo["k2"], n)
                        elif name == "q1":
                            wait(dve, lo["q2"], (b - 2) * HC + part + 1 if blike >= 2 else 0)
                        else:
                            dve.wait_ge(lo["q1"], n)
                        dve.wait_ge(hi[name], n)
                        nc.vector.scalar_tensor_tensor(out=rest[:, part, :], in0=d, scalar=column(name, part),
                                                       in1=parts[name[0]][:, 0, part, :], op0=ALU.add,
                                                       op1=ALU.subtract).then_inc(remains[name], 1)
                        dve.wait_ge(remains[name], n)
                        nc.vector.tensor_copy(parts[name[0]][:, 1, part, :], rest[:, part, :]).then_inc(mid[name], 1)
                    elif name in v_ready:
                        dve.wait_ge(dense_made, made)
                        kind = "self" if name == "v1" else "cross"
                        for t in range(2):
                            dst = v_ones[kind][:, 2 * part + t, 0:NH * VW].rearrange("p (h e) -> p h e", e=VW)[:, :, 0:HD]
                            last = nc.vector.tensor_tensor(
                                dst, d[:, t * H:(t + 1) * H].rearrange("p (h e) -> p h e", e=HD),
                                bias_row(name).rearrange("p (h e) -> p h e", e=HD), ALU.add)
                        last.then_inc(v_ready[name], 1)
                    elif name in sum_ready:
                        h = hidden1 if name == "p1" else hidden2
                        dve.wait_ge(dense_made, made)
                        if part == 0:
                            dve.wait_ge(resid_ready["R1" if name == "p1" else "R2"], b + 1)
                        hv = h[:, 2 * part:2 * part + 2, :].rearrange("p t h -> p (t h)")
                        nc.vector.tensor_tensor(hv, d, hv, ALU.add).then_inc(sum_ready[name], 1)
                        if part == 1:
                            dve.wait_ge(sum_ready[name], 2 * b + 2)
                            if name == "p1":
                                wait(dve, norm_step["t1"], (b + 2) * 4 if blike + 2 <= NB else NB * 4)
                                if blike >= 1:
                                    wait(dve, norm_step["t2"], (b - 1) * 4)
                            else:
                                wait(dve, norm_step["tx"], (b + 2) * 4 if blike + 2 <= NB else NB * 4)
                                wait(dve, norm_step["t1"], (b + 4) * 4 if blike + 4 <= NB else NB * 4)
                            statistics("tx" if name == "p1" else "t2", h, b)
                    elif name == "m":
                        dve.wait_ge(dense_made, made)
                        if part == 0:
                            dve.wait_ge(resid_ready["R3"], b + 1)
                        nc.vector.tensor_tensor(hidden2[:, part, :], d[:, 0:H], hidden2[:, part, :],
                                                ALU.add).then_inc(out_ready, 1)

            iterations(dve, body)

        @block.gpsimd
        def _(pool):
            nc.gpsimd.memset(ident[:], 0.0).then_inc(consts_pool, 1)
            for kind in mask:
                nc.gpsimd.memset(mask[kind][:], 0.0).then_inc(consts_pool, 1)
            pool.wait_ge(consts_pool, 3)
            nc.gpsimd.affine_select(out=ident[:], in_=ident[:], compare_op=ALU.not_equal, fill=1.0, base=0,
                                    pattern=[[-1, P]], channel_multiplier=1).then_inc(consts_pool, 1)
            for kind in mask:
                nc.gpsimd.affine_select(out=mask[kind][:], in_=mask[kind][:], compare_op=ALU.is_ge, fill=NEG,
                                        base=LAST[kind], pattern=[[-1, P + LAST[kind]]],
                                        channel_multiplier=1).then_inc(consts_pool, 1)
            pool.wait_ge(params_loaded, 3 * 16)
            pool.wait_ge(consts_dve, DVE_CONSTS)

            def add_row(dst, src, name):
                return nc.gpsimd.tensor_tensor(dst, src, row[:, ROWS.index(name):ROWS.index(name) + 1, :]
                                               .to_broadcast([P, TB, H]), ALU.add)

            def normalise(name, dst, src, b):
                gate(pool, aggr_ready[name], b + 1)
                nc.gpsimd.tensor_scalar(var_eps[:], mean_var[:, :, 1], EPS, None, ALU.add).then_inc(norm_step[name], 1)
                pool.wait_ge(norm_step[name], b * 4 + 1)
                nc.gpsimd.tensor_tensor(rstd[:], var_eps[:], minus_half[:], ALU.pow).then_inc(norm_step[name], 1)
                pool.wait_ge(norm_step[name], b * 4 + 2)
                nc.gpsimd.tensor_tensor(mean_rstd[:], mean_var[:, :, 0], rstd[:], ALU.mult).then_inc(norm_step[name], 1)
                gate(pool, norm_step[name], b * 4 + 3)
                nc.gpsimd.tensor_scalar(shift[:], mean_rstd[:], -1.0, None, ALU.mult).then_inc(norm_step[name], 1)
                gate(pool, norm_step[name], b * 4 + 4)
                for t in range(TB):
                    nc.gpsimd.tensor_scalar(dst[:, t, :], src[:, t, :], rstd[:, t:t + 1], shift[:, t:t + 1],
                                            ALU.mult, ALU.add).then_inc(norm_ready[name], 1)

            def body(like, i):
                for name, part, blike, b, at, g in items(like, i):
                    if name == "R2":
                        pool.wait_ge(sum_ready["p1"], (b + 1) * 2)
                        wait(pool, out_stored, b * TB * 16)
                        add_row(hidden2[:], hidden1[:], "proj2").then_inc(resid_ready["R2"], 1)
                    elif name == "R1":
                        pool.wait_ge(resid_loaded, (b + 1) * 16)
                        add_row(hidden1[:], hidden1[:], "proj1").then_inc(resid_ready["R1"], 1)
                    elif name == "L1":
                        normalise("t1", x_in, x_in, b)
                    elif name == "p1" and part == 1:
                        wait(pool, turned["t2"], (b - 1) * HC if blike >= 1 else 0)
                        normalise("tx", normed, hidden1, b)
                    elif name == "p2" and part == 1:
                        wait(pool, turned["tx"], (b + 2) * HC if blike + 2 <= NB else NB * HC)
                        normalise("t2", normed, hidden2, b)
                        pool.wait_ge(norm_ready["t2"], (b + 1) * TB)
                        add_row(hidden2[:], hidden2[:], "mlp").then_inc(resid_ready["R3"], 1)
                    elif name in lo:
                        pool.wait_ge(mid[name], b * HC + part + 1)
                        nc.gpsimd.tensor_tensor(parts[name[0]][:, 2, part, :], rest[:, part, :],
                                                parts[name[0]][:, 1, part, :], ALU.subtract).then_inc(lo[name], 1)
                    elif name == "S" and part % 2 == 1:
                        head = g * GH + part
                        gate(pool, exp_done, at.n * NH * 3 + (head + 1) * 3)
                        s0 = (head - 1) % (2 * GH)
                        for kb, (c0, q0, _) in enumerate(prob_cols(at.kind)):
                            v = probs[:, s0:s0 + 2, c0:c0 + P]
                            nc.gpsimd.affine_select(out=v, in_=v, compare_op=ALU.is_ge, fill=0.0,
                                                    base=q0 - kb * P + LAST[at.kind], pattern=[[0, 2], [1, P]],
                                                    channel_multiplier=-1).then_inc(masked, 1)

            iterations(pool, body)


DVE_CONSTS = 7
POOL_CONSTS = 6


def kernel(x, ctx_1024, L0_xattn_scorer_logits, L0_xattn_ln1_g, L0_xattn_ln1_b, L0_xattn_c_attn_w,
           L0_xattn_c_attn_b, L0_xattn_attn_proj_w, L0_xattn_attn_proj_b, L0_xattn_lnx_g, L0_xattn_lnx_b,
           L0_xattn_q_attn_w, L0_xattn_q_attn_b, L0_xattn_x_kv_w, L0_xattn_x_kv_b, L0_xattn_x_proj_w,
           L0_xattn_x_proj_b, L0_xattn_ln2_g, L0_xattn_ln2_b, L0_xattn_fc_w, L0_xattn_fc_b,
           L0_xattn_mlp_proj_w, L0_xattn_mlp_proj_b):
    import concourse.bacc as bacc
    from concourse.bass_utils import run_bass_kernel_spmd

    def split_order(w):
        lead = w.shape[:-1]
        w = w.reshape(*lead, HP, HC, HD)
        return np.moveaxis(w, (-3, -2, -1), (-1, -3, -2)).reshape(*lead, H)

    def by_partition(v):
        return np.reshape(v, (-1, P)).T

    qkv, qkv_b = np.asarray(L0_xattn_c_attn_w), np.asarray(L0_xattn_c_attn_b)
    kv, kv_b = np.asarray(L0_xattn_x_kv_w), np.asarray(L0_xattn_x_kv_b)
    q2, q2_b = np.asarray(L0_xattn_q_attn_w), np.asarray(L0_xattn_q_attn_b)
    columns = {"ln1_g": L0_xattn_ln1_g, "ln1_b": L0_xattn_ln1_b, "lnx_g": L0_xattn_lnx_g,
               "lnx_b": L0_xattn_lnx_b, "ln2_g": L0_xattn_ln2_g, "ln2_b": L0_xattn_ln2_b,
               "q1": split_order(qkv_b[:H]), "k1": split_order(qkv_b[H:2 * H]), "q2": split_order(q2_b),
               "k2": split_order(kv_b[:H]), "fc_b": L0_xattn_fc_b}
    arrays = {
        "in_x": x, "in_ctx": ctx_1024, "in_logits": L0_xattn_scorer_logits,
        "in_w_qkv": np.concatenate([split_order(qkv[:, :H]), split_order(qkv[:, H:2 * H]), qkv[:, 2 * H:]], 1),
        "in_w_proj1": L0_xattn_attn_proj_w,
        "in_w_q2": split_order(q2),
        "in_w_kv2": np.concatenate([split_order(kv[:, :H]), kv[:, H:]], 1),
        "in_w_proj2": L0_xattn_x_proj_w, "in_w_fc": L0_xattn_fc_w, "in_w_mlp": L0_xattn_mlp_proj_w,
        "in_cols": np.concatenate([by_partition(np.asarray(columns[n])) for n in COLS], 1),
        "in_rows": np.stack([qkv_b[2 * H:], np.asarray(L0_xattn_attn_proj_b), kv_b[H:],
                             np.asarray(L0_xattn_x_proj_b), np.asarray(L0_xattn_mlp_proj_b)]),
    }
    arrays = {n: np.ascontiguousarray(a) for n, a in arrays.items()}
    nc = bacc.Bacc("TRN2", target_bir_lowering=False, num_devices=1, dynamic_dma_scratch_size=1024)
    args = [nc.dram_tensor(n, a.shape, mybir.dt.from_np(a.dtype), kind="ExternalInput").ap()
            for n, a in arrays.items()]
    args.append(nc.dram_tensor("out_y", (NB, T, H), F32, kind="ExternalOutput").ap())
    block_kernel(nc, *args)
    return run_bass_kernel_spmd(nc, [arrays], core_ids=[0]).results[0]["out_y"]
```

```python
from contextlib import ExitStack

import numpy as np

import concourse.bass as bass
from concourse import mybir

F32 = mybir.dt.float32
BF16 = mybir.dt.bfloat16
ACT = mybir.ActivationFunctionType
ALU = mybir.AluOpType
AX = mybir.AxisListType

P = 128
NB, T, H = 8, 512, 256
NH = 16
HD = H // NH
INNER = 4 * H
EPS = 1e-5
SCALE = HD ** -0.5
TB = T // P
HC = H // P
FC = INNER // P
GH = 4
NG = NH // GH
HP = NH // HC
VW = HD + 1
VROW = NH * VW + (32 - VW)
NEG = -3.0e38
STACK = 6 * HD
LAST = {"self": 0, "cross": 2}
KMAX = {"self": STACK, "cross": STACK + 3}
KALL = {kind: KMAX[kind] + 2 for kind in KMAX}
PARTS = {"q": (0, 1, 0, 1, 2, 0), "k": (0, 0, 1, 1, 0, 2)}

COLS = {}
for _name, _n in (("ln1_g", HC), ("ln1_b", HC), ("lnx_g", HC), ("lnx_b", HC), ("ln2_g", HC),
                  ("ln2_b", HC), ("q1", HC), ("k1", HC), ("q2", HC), ("k2", HC), ("fc_b", FC)):
    COLS[_name] = (sum(n for _, n in COLS.values()), _n)
NCOL = sum(n for _, n in COLS.values())
ROWS = ("v1", "proj1", "v2", "proj2", "mlp")

TILES = 3
GT = GH * TILES
BEATS = NG * GT
LEAD = GT + 6
PV_AT, ON_AT, MT_AFTER = (3, 4, 5, 6), 10, 2
PLAN = {
    "X": """
        R2 | tc.0 R1 | tc.1 | k2.0 | | k2.1 dk2 | ta1.0 | | ta1.1 | p1.0 | | p1.1 |
        v2.0 | | | v2.1 | | tx.0 | | tx.1 | | q2.0 | | q2.1 dq2 |
        L1 | | | | | | | | t1.0 | | | t1.1 |
        q1.0 | | | q1.1 | | | | | k1.0 | | | k1.1
    """,
    "Y": """
        dq1 dk1 ta2.0 | ta2.1 | p2.0 | p2.1 | | | v1.0 | | v1.1 | | | t2.0 |
        t2.1 | f.0 | f.1 | | f.2 | | f.3 | G.0 | f.4 | f.5 | | f.6 |
        f.7 | G.1 | | | | | | ma.0 | m.0 | | ma.1 | m.1 |
        | | ma.2 | m.2 | | | | ma.3 | m.3 | | |
    """,
}
PLAN = {slot: [beat.split() for beat in text.split("|")] for slot, text in PLAN.items()}
assert all(len(beats) <= BEATS for beats in PLAN.values())
OFFSET = {"L1": 1, "t1": 1, "q1": 1, "k1": 1, "v1": 1, "dq1": 1, "dk1": 1,
          "tc": -1, "k2": -1, "v2": -1, "ta1": -1, "R1": -1, "p1": -1, "tx": -1, "q2": -1, "dq2": -1, "dk2": -1,
          "R2": -2, "ta2": -2, "p2": -2, "t2": -2, "f": -2, "G": -2, "ma": -2, "m": -2}
FIRST, LOOP_FROM, LOOP_TO, END = -1, 3, NB - 1, NB + 2


class Attn:

    def __init__(self, kind, like, i):
        off = 0 if kind == "self" else -1
        self.kind, self.like, self.b = kind, like + off, i + off
        if kind == "self":
            self.n = 0 if self.like == 0 else 2 * self.b - 1
        else:
            self.n = 2 * NB - 1 if self.like == NB - 1 else 2 * self.b + 2


def attention_of(slot, like, i):
    if slot == "X":
        return Attn("self", like, i) if 0 <= like < NB else None
    return Attn("cross", like, i) if 1 <= like <= NB else None


def items(like, i):
    slots = [("Y", like - 1, i - 1), ("X", like, i), ("Y", like, i), ("X", like + 1, i + 1)]
    around = [attention_of(*s) for s in slots]
    for s, slot in ((1, "X"), (2, "Y")):
        def fixed(name, position, part=None):
            at, tile = around[s + position // BEATS], position % BEATS
            if at is not None:
                yield name, tile if part is None else part, at.like, at.b, at, tile // GT

        for beat in range(BEATS):
            yield from fixed("M", beat + LEAD)
            yield from fixed("S", beat)
            if beat % GT in PV_AT:
                yield from fixed("PV", beat - beat % GT - GT, PV_AT.index(beat % GT))
            if (beat + LEAD) % GT == MT_AFTER - 1:
                yield from fixed("MT", beat + LEAD - GT)
            if beat % GT == ON_AT:
                yield from fixed("ON", beat - GT)
            for word in PLAN[slot][beat] if beat < len(PLAN[slot]) else ():
                name, _, part = word.partition(".")
                b = like + OFFSET[name]
                if 0 <= b < NB:
                    yield name, int(part) if part else 0, b, i + OFFSET[name], None, None


def is_dense(name):
    return name not in ("M", "S", "PV", "R1", "R2", "L1", "G", "ma", "dq1", "dk1", "dq2", "dk2")


def dense_count(like):
    return sum(is_dense(item[0]) for item in items(like, like))


PER_LOOP = dense_count(LOOP_FROM)
assert PER_LOOP % 2 == 0
BEFORE = {}
_n = 0
for _like in range(FIRST, END):
    BEFORE[_like] = _n
    _n += dense_count(_like)


MAX_TILES = ((3,), (2,), (1, 0))
EXP_TILES = ((0,), (1,), (2, 3))


def widths(kind):
    return [min(T, P * (q + 1) + LAST[kind]) for q in range(TB)]


def block_kernel(nc, x, ctx, logits, w_qkv, w_proj1, w_q2, w_kv2, w_proj2, w_fc, w_mlp, cols, rows, out):
    with ExitStack() as stack:
        def sb(name, shape, dt=F32):
            return stack.enter_context(nc.sbuf_tensor(name, shape, dt))

        def sem(name):
            return stack.enter_context(nc.semaphore(name))

        max_scores = stack.enter_context(nc.psum_tensor("max_scores", [P, 2, T], F32))
        scores = stack.enter_context(nc.psum_tensor("scores", [P, 3, T], F32))
        pv_out = stack.enter_context(nc.psum_tensor("pv_out", [P, T], F32))
        dense = stack.enter_context(nc.psum_tensor("dense", [P, 2, T], F32))

        qkv_w = sb("qkv_w", [P, HC, 3 * H])
        proj1_w = sb("proj1_w", [P, HC, H])
        q2_w = sb("q2_w", [P, HC, H])
        kv2_w = sb("kv2_w", [P, HC, 2 * H])
        proj2_w = sb("proj2_w", [P, HC, H])
        fc_w = sb("fc_w", [P, HC, INNER])
        mlp_w = sb("mlp_w", [P, FC, H])
        col = sb("col", [P, NCOL])
        row = sb("row", [P, len(ROWS), H])
        ident = sb("ident", [P, P])
        ident_b = sb("ident_b", [P, P], BF16)
        mask = {"self": sb("mask_self", [P, P], BF16), "cross": sb("mask_cross", [P, P + 2], BF16)}
        minus_half = sb("minus_half", [P, TB])

        x_in = sb("x_in", [P, TB, H])
        hidden1 = sb("hidden1", [P, TB, H])
        hidden2 = sb("hidden2", [P, TB, H])
        normed = sb("normed", [P, TB, H])
        attn_out = {"self": sb("attn1", [P, TB, H]), "cross": sb("attn2", [P, TB, H])}
        feat_a = sb("feat_a", [P, HC, T])
        feat_b = sb("feat_b", [P, HC, T])
        inner = sb("inner", [P, FC, T])
        key_bias = inner[0:1, 0, :]
        key_rest = inner[0:1, 1:3, :]
        key_parts = inner[0:1, 3:5, :].bitcast(BF16).rearrange("p a (b t) -> p (a b) t", t=T)
        signs_both = inner[0:3, 5, :].bitcast(BF16)
        signs = {"minus": signs_both[:, 0:T], "plus": signs_both[:, T:2 * T]}
        parts = {s: sb(f"parts_{s}", [P, 3, HC, T], BF16) for s in "qk"}
        rest = {s: sb(f"rest_{s}", [P, HC, T]) for s in "qk"}
        q_stack = {k: sb(f"q_stack_{k}", [KALL[k], NH, T], BF16) for k in KALL}
        k_stack = {k: sb(f"k_stack_{k}", [KALL[k], NH, T], BF16) for k in KALL}
        v_ones = {k: sb(f"v_ones_{k}", [P, TB, VROW]) for k in KALL}
        row_max = sb("row_max", [P, 2, GH * TB])
        max_parts = sb("max_parts", [P, P], BF16)
        max_rows = sb("max_rows", [2 * GH * TB, P], BF16)
        WMAX = sum(widths("cross"))
        probs = sb("probs", [P, 2 * GH, WMAX])
        o_turn = sb("o_turn", [P, T])
        recip = sb("recip", [P, 2, TB, GH])
        stats = sb("stats", [P, TB, 6])
        mean_var = sb("mean_var", [P, TB, 2])
        var_eps = sb("var_eps", [P, TB])
        rstd = sb("rstd", [P, TB])
        mean_rstd = sb("mean_rstd", [P, TB])
        shift = sb("shift", [P, TB])

        qkv_loaded = sem("qkv_loaded")
        weights_loaded = sem("weights_loaded")
        params_loaded = sem("params_loaded")
        consts_pool = sem("consts_pool")
        consts_dve = sem("consts_dve")
        const_rows_loaded = sem("const_rows_loaded")
        bias_rows_loaded = sem("bias_rows_loaded")
        x_loaded = sem("x_loaded")
        ctx_loaded = sem("ctx_loaded")
        resid_loaded = sem("resid_loaded")
        out_stored = sem("out_stored")
        stack_loaded = {n: sem(f"{n}_stacked") for n in ("q1", "k1", "q2", "k2")}
        max_loaded = sem("max_loaded")
        dense_made = sem("dense_made")
        max_scores_made = sem("max_scores_made")
        max_scores_read = sem("max_scores_read")
        scores_made = sem("scores_made")
        exp_done = sem("exp_done")
        masked = sem("masked")
        pv_done = sem("pv_done")
        o_copied = sem("o_copied")
        max_hi = sem("max_hi")
        max_split = sem("max_split")
        max_rows_ready = sem("max_rows_ready")
        recip_ready = sem("recip_ready")
        attn_ready = sem("attn_ready")
        turned = {n: sem(f"{n}_turned") for n in ("t1", "tc", "tx", "t2", "ta1", "ta2")}
        hi = {n: sem(f"{n}_hi") for n in stack_loaded}
        remains = {n: sem(f"{n}_rest") for n in stack_loaded}
        mid = {n: sem(f"{n}_mid") for n in stack_loaded}
        lo = {n: sem(f"{n}_lo") for n in stack_loaded}
        v_ready = {n: sem(f"{n}_ready") for n in ("v1", "v2")}
        sum_ready = {n: sem(f"{n}_sum") for n in ("p1", "p2")}
        inner_ready = sem("inner_ready")
        gelu_ready = sem("gelu_ready")
        out_ready = sem("out_ready")
        resid_ready = {n: sem(f"{n}_added") for n in ("R1", "R2", "R3")}
        stats_ready = {n: sem(f"stats_{n}") for n in ("t1", "tx", "t2")}
        aggr_ready = {n: sem(f"aggr_{n}") for n in ("t1", "tx", "t2")}
        norm_step = {n: sem(f"norm_step_{n}") for n in ("t1", "tx", "t2")}
        norm_ready = {n: sem(f"norm_{n}") for n in ("t1", "tx", "t2")}

        gates_passed = sem("gates_passed")

        block = stack.enter_context(nc.Block())

        def dense_of(like, i):
            if LOOP_FROM <= like < LOOP_TO:
                return BEFORE[LOOP_FROM] + (i - LOOP_FROM) * PER_LOOP
            return BEFORE[like]

        def wait(eng, sem_, value):
            if not (isinstance(value, int) and value <= 0):
                eng.wait_ge(sem_, value)

        def gate(eng, sem_, value):
            eng.wait_ge(sem_, value)
            eng.sem_inc(gates_passed, 1)

        def iterations(eng, body):
            for like in range(FIRST, LOOP_FROM):
                body(like, like)
            with eng.Fori(LOOP_FROM, LOOP_TO) as i:
                body(LOOP_FROM, i)
            for like in range(LOOP_TO, END):
                body(like, like)

        def released(item):
            name, part, _, b, at, g = item
            if name == "MT":
                return max_rows_ready, at.n * NG + g + 1
            if name == "ON":
                return attn_ready, at.n * NG + g + 1
            if name in turned:
                return turned[name], b * HC + part + 1
            if name in remains:
                return remains[name], b * HC + part + 1
            if name in v_ready:
                return v_ready[name], b * 2 + part + 1
            if name in sum_ready:
                return sum_ready[name], b * 2 + part + 1
            if name == "f":
                return inner_ready, b * FC + part + 1
            return out_ready, b * TB + part + 1

        def mask_of(kind, q):
            return mask[kind][:, 0:widths(kind)[q] - P * q]

        def prob_cols(kind):
            at, found = 0, []
            for k in range(TB):
                w = widths(kind)[TB - 1 - k]
                found.append((at, T - w, w))
                at += w
            return found

        @block.sync
        def _(sp):
            sp.dma_start(x_in[:], x[0].rearrange("(t p) h -> p t h", p=P)).then_inc(x_loaded, 16)
            sp.dma_start(col[:], cols).then_inc(params_loaded, 16)
            sp.dma_start(qkv_w[:], w_qkv.rearrange("(c p) n -> p c n", p=P)).then_inc(qkv_loaded, 16)
            sp.dma_start(row[:], rows.partition_broadcast(P)).then_inc(params_loaded, 16)
            sp.dma_start(key_bias[:], logits).then_inc(params_loaded, 16)
            for dst, src in ((proj1_w, w_proj1), (kv2_w, w_kv2), (q2_w, w_q2), (proj2_w, w_proj2),
                             (fc_w, w_fc), (mlp_w, w_mlp)):
                sp.dma_start(dst[:], src.rearrange("(c p) n -> p c n", p=P)).then_inc(weights_loaded, 16)
            sp.wait_ge(consts_pool, POOL_CONSTS)
            for dst, src in ((k_stack["self"][KMAX["self"]:KALL["self"], :, :], signs["minus"][0:2, :]),
                             (k_stack["cross"][KMAX["cross"]:KALL["cross"], :, :], signs["minus"][0:2, :]),
                             (q_stack["cross"][STACK:KMAX["cross"], :, :], signs["plus"][:])):
                sp.dma_start(dst, src.unsqueeze(1).to_broadcast([src.shape[0], NH, T])
                             ).then_inc(const_rows_loaded, 16)
            sp.wait_ge(consts_dve, DVE_CONSTS)
            for r in range(3):
                sp.dma_start(k_stack["cross"][STACK + r:STACK + r + 1, :, :],
                             key_parts[0:1, r:r + 1, :].to_broadcast([1, NH, T])).then_inc(bias_rows_loaded, 16)

            def body(like, i):
                for name, part, blike, b, at, g in items(like, i):
                    if name == "R1":
                        wait(sp, resid_ready["R2"], b)
                        sp.dma_start(hidden1[:], x[b].rearrange("(t p) h -> p t h", p=P)).then_inc(resid_loaded, 16)
                    if name == "tc" and part == HC - 1 and blike + 2 < NB:
                        wait(sp, turned["tc"], (b + 1) * HC)
                        sp.dma_start(x_in[:], x[b + 2].rearrange("(t p) h -> p t h", p=P)).then_inc(x_loaded, 16)
                    if name == "t1" and part == HC - 1 and blike > 0:
                        wait(sp, turned["t1"], (b + 1) * HC)
                        sp.dma_start(x_in[:], ctx[b - 1].rearrange("(t p) h -> p t h", p=P)).then_inc(ctx_loaded, 16)
                    if name[0] == "d":
                        name = name[1:]
                        kind = "self" if name[1] == "1" else "cross"
                        dst = (q_stack if name[0] == "q" else k_stack)[kind]
                        if blike > 0:
                            before = Attn(kind, blike - 1 + (kind == "cross"), b - 1 + (kind == "cross"))
                            wait(sp, scores_made, (before.n + 1) * BEATS)
                        src = parts[name[0]]
                        for p_, ready in ((0, hi), (1, mid), (2, lo)):
                            sp.wait_ge(ready[name], (b + 1) * HC)
                            for r, which in enumerate(PARTS[name[0]]):
                                if which == p_:
                                    sp.dma_start(dst[r * HD:(r + 1) * HD, :, :],
                                                 src[:, p_].rearrange("p c t -> p (c t)")).then_inc(stack_loaded[name], 16)
                    if name == "MT":
                        sp.wait_ge(max_rows_ready, at.n * NG + g + 1)
                        sp.dma_start(q_stack[at.kind][KMAX[at.kind]:KALL[at.kind], g * GH:(g + 1) * GH, :],
                                     max_rows[:]).then_inc(max_loaded, 16)
                    if name == "m":
                        sp.wait_ge(out_ready, b * TB + part + 1)
                        sp.dma_start(out[b, part * P:(part + 1) * P, :], hidden2[:, part, :]).then_inc(out_stored, 16)
                if like == NB - 1:
                    sp.wait_ge(turned["tc"], (NB - 1) * HC)
                    sp.dma_start(x_in[:], ctx[NB - 1].rearrange("(t p) h -> p t h", p=P)).then_inc(ctx_loaded, 16)

            body(FIRST, FIRST)
            sp.wait_ge(turned["t1"], HC)
            sp.dma_start(x_in[:], x[1].rearrange("(t p) h -> p t h", p=P)).then_inc(x_loaded, 16)
            for like in range(FIRST + 1, LOOP_FROM):
                body(like, like)
            with sp.Fori(LOOP_FROM, LOOP_TO) as i:
                body(LOOP_FROM, i)
            for like in range(LOOP_TO, END):
                body(like, like)
            sp.wait_ge(out_stored, NB * TB * 16)

        @block.tensor
        def _(pe):
            pe.wait_ge(consts_pool, POOL_CONSTS)
            pe.wait_ge(qkv_loaded, 16)

            def turn(dst, src, part):
                for t in range(TB):
                    last = pe.transpose(dst[:, t * P:(t + 1) * P], src[:, t, part * P:(part + 1) * P], ident[:])
                return last

            def by_feature(dst, w, at, src):
                for c in range(HC):
                    last = pe.matmul(dst, w[:, c, at:at + P], src[:, c, :], start=(c == 0), stop=(c == HC - 1))
                return last

            def by_token(dst, src, w, at, t, some=range(HC), chunks=HC):
                for c in some:
                    last = pe.matmul(dst, src[:, c, t * P:(t + 1) * P], w[:, c, at:at + H],
                                     start=(c == 0), stop=(c == chunks - 1))
                return last

            def body(like, i):
                k = 0
                recent = [x_ for x_ in items(like - 1, i - 1) if is_dense(x_[0])] if like > FIRST else []

                def claim():
                    if len(recent) >= 2:
                        wait(pe, *released(recent[-2]))
                    return (BEFORE[like] + k) % 2

                for item in items(like, i):
                    name, part, blike, b, at, g = item
                    if name == "M":
                        head, r = part // TILES, part % TILES
                        if part == 0:
                            n = "1" if at.kind == "self" else "2"
                            pe.wait_ge(stack_loaded["q" + n], (at.b + 1) * 6 * 16)
                            pe.wait_ge(stack_loaded["k" + n], (at.b + 1) * 6 * 16)
                            if at.kind == "self" and at.like == 0:
                                pe.wait_ge(const_rows_loaded, 3 * 16)
                                pe.wait_ge(consts_dve, 1)
                            if at.kind == "cross" and at.like == 0:
                                pe.wait_ge(bias_rows_loaded, 3 * 16)
                        rows_ = KMAX[at.kind]
                        W = widths(at.kind)
                        bank = part % 2
                        wait(pe, max_scores_read, at.n * BEATS + part - 1)
                        c0 = 0
                        for q in MAX_TILES[r]:
                            pe.matmul(max_scores[:, bank, c0:c0 + W[q]],
                                      q_stack[at.kind][0:rows_, head, q * P:(q + 1) * P],
                                      k_stack[at.kind][0:rows_, head, 0:W[q]], start=True, stop=False)
                            last = pe.matmul(max_scores[:, bank, c0 + q * P:c0 + W[q]], ident_b[:],
                                             mask_of(at.kind, q), start=False, stop=True)
                            c0 += W[q]
                        last.then_inc(max_scores_made, 1)
                    elif name == "S":
                        head, r = part // TILES, part % TILES
                        if part % GT == 0:
                            pe.wait_ge(max_loaded, (at.n * NG + g + 1) * 16)
                        rows_ = KALL[at.kind]
                        wait(pe, exp_done, at.n * BEATS + part - 2)
                        c0 = 0
                        for kb in EXP_TILES[r]:
                            _, q0, w = prob_cols(at.kind)[kb]
                            last = pe.matmul(scores[:, r, c0:c0 + w],
                                             k_stack[at.kind][0:rows_, head, kb * P:(kb + 1) * P],
                                             q_stack[at.kind][0:rows_, head, q0:T], start=True, stop=True)
                            c0 += w
                        last.then_inc(scores_made, 1)
                    elif name == "PV":
                        if part == 0:
                            pe.wait_ge(masked, at.n * NH * 2 + (g + 1) * GH * 2)
                            if g == 0:
                                pe.wait_ge(v_ready["v1" if at.kind == "self" else "v2"], (at.b + 1) * 2)
                        c0, q0, w = prob_cols(at.kind)[part]
                        for j in range(GH):
                            head = g * GH + j
                            last = pe.matmul(pv_out[32 * j:32 * j + 32, q0:T],
                                             v_ones[at.kind][:, part, head * VW:head * VW + 32],
                                             probs[:, head % (2 * GH), c0:c0 + w],
                                             start=(part == 0), stop=(part == TB - 1))
                        if part == TB - 1:
                            last.then_inc(pv_done, 1)
                    if name == "ma":
                        bank = claim()
                        pe.wait_ge(gelu_ready, (b + 1) * 2)
                        by_token(dense[:, bank, 0:H], inner, mlp_w, 0, part, range(FC // 2), FC)
                    if not is_dense(name):
                        continue
                    bank = (BEFORE[like] + k) % 2 if name == "m" else claim()
                    recent.append(item)
                    k += 1
                    d = dense[:, bank, :]
                    if name == "MT":
                        pe.wait_ge(max_split, at.n * NG + g + 1)
                        last = pe.transpose(d.bitcast(BF16)[:, 0:P], max_parts[:], ident_b[:])
                    elif name == "ON":
                        pe.wait_ge(o_copied, at.n * NG + g + 1)
                        for t in range(TB):
                            last = pe.transpose(d[:, t * P:(t + 1) * P], o_turn[:, t * P:(t + 1) * P], ident[:])
                    elif name in ("t1", "tx", "t2"):
                        pe.wait_ge(norm_ready[name], (b + 1) * TB)
                        last = turn(d, x_in if name == "t1" else normed, part)
                    elif name == "tc":
                        pe.wait_ge(ctx_loaded, (b + 1) * 16)
                        last = turn(d, x_in, part)
                    elif name in ("ta1", "ta2"):
                        kind = "self" if name == "ta1" else "cross"
                        a = Attn(kind, blike + (kind == "cross"), b + (kind == "cross"))
                        pe.wait_ge(attn_ready, (a.n + 1) * NG)
                        last = turn(d, attn_out[kind], part)
                    elif name in ("q1", "k1"):
                        pe.wait_ge(turned["t1"], (b + 1) * HC)
                        last = by_feature(d, qkv_w, (name == "k1") * H + part * P, feat_a)
                    elif name == "q2":
                        pe.wait_ge(turned["tx"], (b + 1) * HC)
                        last = by_feature(d, q2_w, part * P, feat_b)
                    elif name == "k2":
                        pe.wait_ge(turned["tc"], (b + 1) * HC)
                        last = by_feature(d, kv2_w, part * P, feat_a)
                    elif name in ("v1", "v2"):
                        pe.wait_ge(turned["t1" if name == "v1" else "tc"], (b + 1) * HC)
                        w, c0 = (qkv_w, 2 * H) if name == "v1" else (kv2_w, H)
                        for t in range(2):
                            last = by_token(d[:, t * H:(t + 1) * H], feat_a, w, c0, 2 * part + t)
                    elif name in ("p1", "p2"):
                        pe.wait_ge(turned["ta1" if name == "p1" else "ta2"], (b + 1) * HC)
                        for t in range(2):
                            last = by_token(d[:, t * H:(t + 1) * H], feat_b,
                                            proj1_w if name == "p1" else proj2_w, 0, 2 * part + t)
                    elif name == "f":
                        pe.wait_ge(turned["t2"], (b + 1) * HC)
                        last = by_feature(d, fc_w, part * P, feat_b)
                    else:
                        last = by_token(d[:, 0:H], inner, mlp_w, 0, part, range(FC // 2, FC), FC)
                    last.then_inc(dense_made, 1)
                if like == FIRST:
                    pe.wait_ge(weights_loaded, 6 * 16)

            iterations(pe, body)

        @block.scalar
        def _(act):
            act.wait_ge(params_loaded, 3 * 16)

            def column(name, part):
                at = COLS[name][0] + part
                return col[:, at:at + 1]

            def body(like, i):
                made = dense_of(like, i)
                for name, part, blike, b, at, g in items(like, i):
                    if is_dense(name):
                        made = made + 1
                        d = dense[:, (BEFORE[like] + is_first[0]) % 2, :]
                        is_first[0] += 1
                    if name == "S":
                        head, r = part // TILES, part % TILES
                        if part % GT == 0:
                            wait(act, pv_done, at.n * NG + g - 1)
                        cols_ = prob_cols(at.kind)
                        c0, w = cols_[EXP_TILES[r][0]][0], sum(cols_[kb][2] for kb in EXP_TILES[r])
                        act.wait_ge(scores_made, at.n * BEATS + part + 1)
                        nc.scalar.activation(probs[:, head % (2 * GH), c0:c0 + w], scores[:, r, 0:w],
                                             ACT.Exp, scale=SCALE).then_inc(exp_done, 1)
                    elif name == "PV" and part == TB - 1:
                        act.wait_ge(pv_done, at.n * NG + g + 1)
                        nc.scalar.copy(o_turn[:], pv_out[:]).then_inc(o_copied, 1)
                    elif name in ("t1", "tx", "t2"):
                        ln = {"t1": "ln1", "tx": "lnx", "t2": "ln2"}[name]
                        act.wait_ge(dense_made, made)
                        nc.scalar.activation((feat_a if name == "t1" else feat_b)[:, part, :], d, ACT.Identity,
                                             bias=column(ln + "_b", part), scale=column(ln + "_g", part)
                                             ).then_inc(turned[name], 1)
                    elif name in ("tc", "ta1", "ta2"):
                        act.wait_ge(dense_made, made)
                        nc.scalar.copy((feat_a if name == "tc" else feat_b)[:, part, :], d).then_inc(turned[name], 1)
                    elif name in hi:
                        if part == 0:
                            if name[1] == "1":
                                wait(act, stack_loaded[name[0] + "2"], (b - 1) * 96 if blike >= 2 else 0)
                            else:
                                wait(act, stack_loaded[name[0] + "1"], (b + 2) * 96 if blike + 2 <= NB else NB * 96)
                        act.wait_ge(dense_made, made)
                        nc.scalar.activation(parts[name[0]][:, 0, part, :], d, ACT.Identity,
                                             bias=column(name, part)).then_inc(hi[name], 1)
                    elif name == "f":
                        act.wait_ge(dense_made, made)
                        nc.scalar.activation(inner[:, part, :], d, ACT.Identity,
                                             bias=column("fc_b", part)).then_inc(inner_ready, 1)
                    elif name == "G":
                        act.wait_ge(inner_ready, b * FC + (part + 1) * FC // 2)
                        v = inner[:, part * FC // 2:(part + 1) * FC // 2, :]
                        nc.scalar.activation(v, v, ACT.Gelu_apprx_tanh).then_inc(gelu_ready, 1)

            is_first = [0]

            def counted(like, i):
                is_first[0] = 0
                body(like, i)

            iterations(act, counted)

        @block.vector
        def _(dve):
            for kind in KALL:
                nc.vector.memset(v_ones[kind][:], 1.0)
            nc.vector.memset(max_parts[:], 0.0)
            dve.wait_ge(consts_pool, POOL_CONSTS)
            nc.vector.tensor_copy(ident_b[:], ident[:]).then_inc(consts_dve, 1)
            dve.wait_ge(params_loaded, 3 * 16)
            steps = (
                lambda: nc.vector.tensor_scalar_mul(key_bias[:], key_bias[:], 1.0 / SCALE),
                lambda: nc.vector.tensor_copy(key_parts[:, 0, :], key_bias[:]),
                lambda: nc.vector.tensor_tensor(key_rest[:, 0, :], key_bias[:], key_parts[:, 0, :], ALU.subtract),
                lambda: nc.vector.tensor_copy(key_parts[:, 1, :], key_rest[:, 0, :]),
                lambda: nc.vector.tensor_tensor(key_rest[:, 1, :], key_rest[:, 0, :], key_parts[:, 1, :], ALU.subtract),
                lambda: nc.vector.tensor_copy(key_parts[:, 2, :], key_rest[:, 1, :]),
            )
            for n, step in enumerate(steps):
                if n:
                    dve.wait_ge(consts_dve, n + 1)
                step().then_inc(consts_dve, 1)

            def column(name, part):
                at = COLS[name][0] + part
                return col[:, at:at + 1]

            def bias_row(name):
                return row[:, ROWS.index(name), :]

            def statistics(name, src, b):
                for t in range(TB):
                    last = nc.vector.bn_stats(stats[:, t, :], src[:, t, :])
                last.then_inc(stats_ready[name], 1)
                gate(dve, stats_ready[name], b + 1)
                for t in range(TB):
                    last = nc.vector.bn_aggr(mean_var[:, t, :], stats[:, t, :])
                last.then_inc(aggr_ready[name], 1)

            def body(like, i):
                made, k = dense_of(like, i), 0
                for name, part, blike, b, at, g in items(like, i):
                    if is_dense(name):
                        made = made + 1
                        d = dense[:, (BEFORE[like] + k) % 2, :]
                        k += 1
                    if name == "L1":
                        dve.wait_ge(x_loaded, (b + 1) * 16)
                        if blike >= 3:
                            dve.wait_ge(norm_step["t2"], (b - 3) * 4)
                        if blike >= 2:
                            dve.wait_ge(norm_step["tx"], (b - 1) * 4)
                        statistics("t1", x_in, b)
                    elif name == "M":
                        j, r = part // TILES % GH, part % TILES
                        W = widths(at.kind)
                        dve.wait_ge(max_scores_made, at.n * BEATS + part + 1)
                        c0 = 0
                        for q in MAX_TILES[r]:
                            c = j * TB + q
                            last = nc.vector.tensor_reduce(row_max[:, g % 2, c:c + 1],
                                                           max_scores[:, part % 2, c0:c0 + W[q]],
                                                           AX.X, ALU.max)
                            c0 += W[q]
                        last.then_inc(max_scores_read, 1)
                        if part % GT == GT - 1:
                            n = GH * TB
                            dve.wait_ge(max_scores_read, at.n * BEATS + (g + 1) * GT)
                            nc.vector.tensor_copy(max_parts[:, 0:n], row_max[:, g % 2, :]).then_inc(max_hi, 1)
                            dve.wait_ge(max_hi, at.n * NG + g + 1)
                            nc.vector.tensor_tensor(max_parts[:, n:2 * n], row_max[:, g % 2, :], max_parts[:, 0:n],
                                                    ALU.subtract).then_inc(max_split, 1)
                    elif name == "MT":
                        dve.wait_ge(dense_made, made)
                        wait(dve, max_loaded, (at.n * NG + g) * 16)
                        nc.vector.tensor_copy(max_rows[:], d.bitcast(BF16)[0:2 * GH * TB, 0:P]).then_inc(max_rows_ready, 1)
                    elif name == "ON":
                        o = d.rearrange("p (q h e) -> p q h e", q=TB, h=GH)
                        dve.wait_ge(dense_made, made)
                        nc.vector.reciprocal(recip[:, g % 2], o[:, :, :, HD]).then_inc(recip_ready, 1)
                        dve.wait_ge(recip_ready, at.n * NG + g + 1)
                        dst = attn_out[at.kind][:, :, g * GH * HD:(g + 1) * GH * HD]
                        nc.vector.tensor_tensor(dst.rearrange("p q (h e) -> p q h e", h=GH), o[:, :, :, 0:HD],
                                                recip[:, g % 2].unsqueeze(3).to_broadcast([P, TB, GH, HD]),
                                                ALU.mult).then_inc(attn_ready, 1)
                    elif name in hi:
                        n = b * HC + part + 1
                        if name[1] == "2":
                            wait(dve, lo[name[0] + "1"], (b + 1) * HC + part + 1 if blike + 1 < NB else NB * HC - HC + part + 1)
                        else:
                            wait(dve, lo[name[0] + "2"], (b - 2) * HC + part + 1 if blike >= 2 else 0)
                        dve.wait_ge(hi[name], n)
                        nc.vector.scalar_tensor_tensor(out=rest[name[0]][:, part, :], in0=d, scalar=column(name, part),
                                                       in1=parts[name[0]][:, 0, part, :], op0=ALU.add,
                                                       op1=ALU.subtract).then_inc(remains[name], 1)
                        dve.wait_ge(remains[name], n)
                        nc.vector.tensor_copy(parts[name[0]][:, 1, part, :], rest[name[0]][:, part, :]).then_inc(mid[name], 1)
                    elif name in v_ready:
                        dve.wait_ge(dense_made, made)
                        kind = "self" if name == "v1" else "cross"
                        for t in range(2):
                            dst = v_ones[kind][:, 2 * part + t, 0:NH * VW].rearrange("p (h e) -> p h e", e=VW)[:, :, 0:HD]
                            last = nc.vector.tensor_tensor(
                                dst, d[:, t * H:(t + 1) * H].rearrange("p (h e) -> p h e", e=HD),
                                bias_row(name).rearrange("p (h e) -> p h e", e=HD), ALU.add)
                        last.then_inc(v_ready[name], 1)
                    elif name in sum_ready:
                        h = hidden1 if name == "p1" else hidden2
                        dve.wait_ge(dense_made, made)
                        if part == 0:
                            dve.wait_ge(resid_ready["R1" if name == "p1" else "R2"], b + 1)
                        hv = h[:, 2 * part:2 * part + 2, :].rearrange("p t h -> p (t h)")
                        nc.vector.tensor_tensor(hv, d, hv, ALU.add).then_inc(sum_ready[name], 1)
                        if part == 1:
                            dve.wait_ge(sum_ready[name], 2 * b + 2)
                            if name == "p1":
                                wait(dve, norm_step["t1"], (b + 2) * 4 if blike + 2 <= NB else NB * 4)
                                if blike >= 1:
                                    wait(dve, norm_step["t2"], (b - 1) * 4)
                            else:
                                wait(dve, norm_step["tx"], (b + 2) * 4 if blike + 2 <= NB else NB * 4)
                                wait(dve, norm_step["t1"], (b + 4) * 4 if blike + 4 <= NB else NB * 4)
                            statistics("tx" if name == "p1" else "t2", h, b)
                    elif name == "m":
                        dve.wait_ge(dense_made, made)
                        if part == 0:
                            dve.wait_ge(resid_ready["R3"], b + 1)
                        nc.vector.tensor_tensor(hidden2[:, part, :], d[:, 0:H], hidden2[:, part, :],
                                                ALU.add).then_inc(out_ready, 1)

            iterations(dve, body)

        @block.gpsimd
        def _(pool):
            nc.gpsimd.memset(ident[:], 0.0).then_inc(consts_pool, 1)
            for kind in mask:
                nc.gpsimd.memset(mask[kind][:], 0.0).then_inc(consts_pool, 1)
            nc.gpsimd.memset(minus_half[:], -0.5).then_inc(consts_pool, 1)
            nc.gpsimd.memset(signs["minus"][:], -1.0).then_inc(consts_pool, 1)
            nc.gpsimd.memset(signs["plus"][:], 1.0).then_inc(consts_pool, 1)
            pool.wait_ge(consts_pool, 6)
            nc.gpsimd.affine_select(out=ident[:], in_=ident[:], compare_op=ALU.not_equal, fill=1.0, base=0,
                                    pattern=[[-1, P]], channel_multiplier=1).then_inc(consts_pool, 1)
            for kind in mask:
                nc.gpsimd.affine_select(out=mask[kind][:], in_=mask[kind][:], compare_op=ALU.is_ge, fill=NEG,
                                        base=LAST[kind], pattern=[[-1, P + LAST[kind]]],
                                        channel_multiplier=1).then_inc(consts_pool, 1)
            pool.wait_ge(consts_pool, POOL_CONSTS)
            pool.wait_ge(params_loaded, 3 * 16)

            def add_row(dst, src, name):
                return nc.gpsimd.tensor_tensor(dst, src, row[:, ROWS.index(name):ROWS.index(name) + 1, :]
                                               .to_broadcast([P, TB, H]), ALU.add)

            def normalise(name, dst, src, b):
                gate(pool, aggr_ready[name], b + 1)
                nc.gpsimd.tensor_scalar(var_eps[:], mean_var[:, :, 1], EPS, None, ALU.add).then_inc(norm_step[name], 1)
                pool.wait_ge(norm_step[name], b * 4 + 1)
                nc.gpsimd.tensor_tensor(rstd[:], var_eps[:], minus_half[:], ALU.pow).then_inc(norm_step[name], 1)
                pool.wait_ge(norm_step[name], b * 4 + 2)
                nc.gpsimd.tensor_tensor(mean_rstd[:], mean_var[:, :, 0], rstd[:], ALU.mult).then_inc(norm_step[name], 1)
                gate(pool, norm_step[name], b * 4 + 3)
                nc.gpsimd.tensor_scalar(shift[:], mean_rstd[:], -1.0, None, ALU.mult).then_inc(norm_step[name], 1)
                gate(pool, norm_step[name], b * 4 + 4)
                for t in range(TB):
                    nc.gpsimd.tensor_scalar(dst[:, t, :], src[:, t, :], rstd[:, t:t + 1], shift[:, t:t + 1],
                                            ALU.mult, ALU.add).then_inc(norm_ready[name], 1)

            def body(like, i):
                for name, part, blike, b, at, g in items(like, i):
                    if name == "R2":
                        pool.wait_ge(sum_ready["p1"], (b + 1) * 2)
                        wait(pool, out_stored, b * TB * 16)
                        add_row(hidden2[:], hidden1[:], "proj2").then_inc(resid_ready["R2"], 1)
                    elif name == "R1":
                        pool.wait_ge(resid_loaded, (b + 1) * 16)
                        add_row(hidden1[:], hidden1[:], "proj1").then_inc(resid_ready["R1"], 1)
                    elif name == "L1":
                        normalise("t1", x_in, x_in, b)
                    elif name == "p1" and part == 1:
                        wait(pool, turned["t2"], (b - 1) * HC if blike >= 1 else 0)
                        normalise("tx", normed, hidden1, b)
                    elif name == "p2" and part == 1:
                        wait(pool, turned["tx"], (b + 2) * HC if blike + 2 <= NB else NB * HC)
                        normalise("t2", normed, hidden2, b)
                        pool.wait_ge(norm_ready["t2"], (b + 1) * TB)
                        add_row(hidden2[:], hidden2[:], "mlp").then_inc(resid_ready["R3"], 1)
                    elif name in lo:
                        pool.wait_ge(mid[name], b * HC + part + 1)
                        nc.gpsimd.tensor_tensor(parts[name[0]][:, 2, part, :], rest[name[0]][:, part, :],
                                                parts[name[0]][:, 1, part, :], ALU.subtract).then_inc(lo[name], 1)
                    elif name == "S" and part % (2 * TILES) == 2 * TILES - 1:
                        head = part // TILES
                        gate(pool, exp_done, at.n * BEATS + part + 1)
                        s0 = (head - 1) % (2 * GH)
                        for kb, (c0, q0, _) in enumerate(prob_cols(at.kind)):
                            v = probs[:, s0:s0 + 2, c0:c0 + P]
                            nc.gpsimd.affine_select(out=v, in_=v, compare_op=ALU.is_ge, fill=0.0,
                                                    base=q0 - kb * P + LAST[at.kind], pattern=[[0, 2], [1, P]],
                                                    channel_multiplier=-1).then_inc(masked, 1)

            iterations(pool, body)


DVE_CONSTS = 7
POOL_CONSTS = 9


def kernel(x, ctx_1024, L0_xattn_scorer_logits, L0_xattn_ln1_g, L0_xattn_ln1_b, L0_xattn_c_attn_w,
           L0_xattn_c_attn_b, L0_xattn_attn_proj_w, L0_xattn_attn_proj_b, L0_xattn_lnx_g, L0_xattn_lnx_b,
           L0_xattn_q_attn_w, L0_xattn_q_attn_b, L0_xattn_x_kv_w, L0_xattn_x_kv_b, L0_xattn_x_proj_w,
           L0_xattn_x_proj_b, L0_xattn_ln2_g, L0_xattn_ln2_b, L0_xattn_fc_w, L0_xattn_fc_b,
           L0_xattn_mlp_proj_w, L0_xattn_mlp_proj_b):
    import concourse.bacc as bacc
    from concourse.bass_utils import run_bass_kernel_spmd

    def split_order(w):
        lead = w.shape[:-1]
        w = w.reshape(*lead, HP, HC, HD)
        return np.moveaxis(w, (-3, -2, -1), (-1, -3, -2)).reshape(*lead, H)

    def by_partition(v):
        return np.reshape(v, (-1, P)).T

    qkv, qkv_b = np.asarray(L0_xattn_c_attn_w), np.asarray(L0_xattn_c_attn_b)
    kv, kv_b = np.asarray(L0_xattn_x_kv_w), np.asarray(L0_xattn_x_kv_b)
    q2, q2_b = np.asarray(L0_xattn_q_attn_w), np.asarray(L0_xattn_q_attn_b)
    columns = {"ln1_g": L0_xattn_ln1_g, "ln1_b": L0_xattn_ln1_b, "lnx_g": L0_xattn_lnx_g,
               "lnx_b": L0_xattn_lnx_b, "ln2_g": L0_xattn_ln2_g, "ln2_b": L0_xattn_ln2_b,
               "q1": split_order(qkv_b[:H]), "k1": split_order(qkv_b[H:2 * H]), "q2": split_order(q2_b),
               "k2": split_order(kv_b[:H]), "fc_b": L0_xattn_fc_b}
    arrays = {
        "in_x": x, "in_ctx": ctx_1024, "in_logits": L0_xattn_scorer_logits,
        "in_w_qkv": np.concatenate([split_order(qkv[:, :H]), split_order(qkv[:, H:2 * H]), qkv[:, 2 * H:]], 1),
        "in_w_proj1": L0_xattn_attn_proj_w,
        "in_w_q2": split_order(q2),
        "in_w_kv2": np.concatenate([split_order(kv[:, :H]), kv[:, H:]], 1),
        "in_w_proj2": L0_xattn_x_proj_w, "in_w_fc": L0_xattn_fc_w, "in_w_mlp": L0_xattn_mlp_proj_w,
        "in_cols": np.concatenate([by_partition(np.asarray(columns[n])) for n in COLS], 1),
        "in_rows": np.stack([qkv_b[2 * H:], np.asarray(L0_xattn_attn_proj_b), kv_b[H:],
                             np.asarray(L0_xattn_x_proj_b), np.asarray(L0_xattn_mlp_proj_b)]),
    }
    arrays = {n: np.ascontiguousarray(a) for n, a in arrays.items()}
    nc = bacc.Bacc("TRN2", target_bir_lowering=False, num_devices=1, dynamic_dma_scratch_size=1024)
    args = [nc.dram_tensor(n, a.shape, mybir.dt.from_np(a.dtype), kind="ExternalInput").ap()
            for n, a in arrays.items()]
    args.append(nc.dram_tensor("out_y", (NB, T, H), F32, kind="ExternalOutput").ap())
    block_kernel(nc, *args)
    return run_bass_kernel_spmd(nc, [arrays], core_ids=[0]).results[0]["out_y"]
```

```python
from contextlib import ExitStack

import numpy as np

import concourse.bass as bass
from concourse import mybir

F32 = mybir.dt.float32
BF16 = mybir.dt.bfloat16
ACT = mybir.ActivationFunctionType
ALU = mybir.AluOpType
AX = mybir.AxisListType

P = 128
NB, T, H = 8, 512, 256
NH = 16
HD = H // NH
INNER = 4 * H
EPS = 1e-5
SCALE = HD ** -0.5
TB = T // P
HC = H // P
FC = INNER // P
GH = 4
NG = NH // GH
HP = NH // HC
VW = HD + 1
VROW = NH * VW + (32 - VW)
NEG = -3.0e38
STACK = 6 * HD
LAST = {"self": 0, "cross": 2}
KMAX = {"self": STACK, "cross": STACK + 3}
KALL = {kind: KMAX[kind] + 2 for kind in KMAX}
PARTS = {"q": (0, 1, 0, 1, 2, 0), "k": (0, 0, 1, 1, 0, 2)}

COLS = {}
for _name, _n in (("ln1_g", HC), ("ln1_b", HC), ("lnx_g", HC), ("lnx_b", HC), ("ln2_g", HC),
                  ("ln2_b", HC), ("q1", HC), ("k1", HC), ("q2", HC), ("k2", HC), ("fc_b", FC)):
    COLS[_name] = (sum(n for _, n in COLS.values()), _n)
NCOL = sum(n for _, n in COLS.values())
ROWS = ("v1", "proj1", "v2", "proj2", "mlp")

TILES = 3
GT = GH * TILES
BEATS = NG * GT
LEAD = GT + 6
PV_AT, ON_AT, MT_AFTER = (3, 4, 5, 6), 10, 2
MAX_BANKS, EXP_BANKS = 3, 2
PLAN = {
    "X": """0:dq2,dk2 1:L1 2:ma.3 4:m.3 7:v2.0 9:v2.1 11:t1.0 12:ta2.0 13:ta2.1 14:t1.1 15:p2.0 17:p2.1
            18:R2 19:q1.0 21:q1.1 24:k1.0 26:k1.1 28:t2.0 29:t2.1 31:f.0 33:f.1 35:f.2 38:f.3 39:G.0
            41:f.4 43:f.5 46:f.6""",
    "Y": """0:dq1,dk1 0:f.7 0:dR 2:G.1 4:R1 7:v1.0 9:v1.1 11:tc.0,ta1.0 12:tc.1,ta1.1 14:p1.0 16:p1.1
            18:k2.0 20:k2.1 22:ma.0 24:m.0 26:tx.0 27:tx.1 29:q2.0 32:q2.1 35:ma.1 37:m.1 43:ma.2 45:m.2""",
}
UNUSUAL = {
    ("Y", 0): "0:dq1,dk1 0:dR 7:v1.0 9:v1.1",
    ("X", 1): """0:tc.0<,tc.1< 0:R1< 1:ta1.0< 2:ta1.1< 4:p1.0< 5:p1.1< 7:k2.0< 9:k2.1< 12:v2.0 14:v2.1
                 16:tx.0< 17:tx.1< 19:q2.0< 21:q2.1<,dq2,dk2 20:L1 22:R2 27:t1.0 28:t1.1 30:q1.0 33:q1.1
                 36:k1.0 39:k1.1""",
    ("X", NB): """0:dq2,dk2 2:ma.3 4:m.3 7:v2.0 9:v2.1 12:ta2.0 13:ta2.1 15:p2.0 17:p2.1 18:R2 34:t2.0 35:t2.1
                  37:f.0 39:f.1 42:f.2 45:f.3 46:G.0""",
    ("Y", NB): """0:f.4 4:f.5 7:f.6 9:f.7 11:G.1 13:ma.0 15:m.0 19:ma.1 21:m.1 25:ma.2 27:m.2 31:ma.3 33:m.3""",
    ("X", NB + 1): "12:ta2.0,ta2.1,p2.0,p2.1,t2.0,t2.1,f.0,f.1,f.2,f.3,G.0,f.4,f.5,f.6,f.7",
    ("Y", NB + 1): "0:G.1,ma.0,m.0,ma.1,m.1,ma.2,m.2,ma.3,m.3",
}
OFFSET = {"L1": 1, "t1": 1, "q1": 1, "k1": 1, "v1": 1, "dq1": 1, "dk1": 1,
          "tc": 0, "k2": 0, "ta1": 0, "dR": 0, "R1": 0, "p1": 0, "tx": 0, "q2": 0,
          "v2": -1, "R2": -1, "dq2": -1, "dk2": -1,
          "ta2": -2, "p2": -2, "t2": -2, "f": -2, "G": -2, "ma": -2, "m": -2}
FIRST, LOOP_FROM, LOOP_TO, END = -1, 3, NB - 2, NB + 2


def planned(slot, like, i):
    beats = [[] for _ in range(BEATS)]
    for word in UNUSUAL.get((slot, like), PLAN[slot]).split():
        beat, _, names = word.partition(":")
        for name in names.split(","):
            off = -1 if name.endswith("<") else 0
            name, _, part = name.rstrip("<").partition(".")
            off += OFFSET[name]
            if name in ("ma", "m") and part == "3" and slot == "X":
                off -= 1
            if 0 <= like + off < NB:
                beats[int(beat)].append((name, int(part or 0), like + off, i + off))
    return beats


TP = 2


def other(name):
    return name[0] + ("2" if name[1] == "1" else "1")


class Attn:

    def __init__(self, kind, like, i):
        off = 0 if kind == "self" else -1
        self.kind, self.like, self.b = kind, like + off, i + off
        if kind == "self":
            self.n = 0 if self.like == 0 else 2 * self.b - 1
        else:
            self.n = 2 * NB - 1 if self.like == NB - 1 else 2 * self.b + 2


def attention_of(slot, like, i):
    if slot == "X":
        return Attn("self", like, i) if 0 <= like < NB else None
    return Attn("cross", like, i) if 1 <= like <= NB else None


def items(like, i):
    slots = [("Y", like - 1, i - 1), ("X", like, i), ("Y", like, i), ("X", like + 1, i + 1)]
    around = [attention_of(*s) for s in slots]
    for s, slot in ((1, "X"), (2, "Y")):
        def fixed(name, position, part=None):
            at, tile = around[s + position // BEATS], position % BEATS
            if at is not None:
                yield name, tile if part is None else part, at.like, at.b, at, tile // GT

        plan = planned(slot, like, i)
        for beat in range(BEATS):
            yield from fixed("M", beat + LEAD)
            yield from fixed("S", beat)
            if beat % GT in PV_AT:
                yield from fixed("PV", beat - beat % GT - GT, PV_AT.index(beat % GT))
            if (beat + LEAD) % GT == MT_AFTER - 1:
                yield from fixed("MT", beat + LEAD - GT)
            if beat % GT == ON_AT:
                yield from fixed("ON", beat - GT)
            for name, part, blike, b in plan[beat]:
                yield name, part, blike, b, None, None


def is_dense(name):
    return name not in ("M", "S", "PV", "R1", "R2", "L1", "G", "ma", "dR", "dq1", "dk1", "dq2", "dk2")


STARTED, BEFORE, _count = {}, {}, {}
for _like in range(FIRST, END + 1):
    STARTED[_like] = dict(_count)
    BEFORE[_like] = sum(n for key, n in _count.items() if "." not in key and is_dense(key))
    for _item in items(_like, _like) if _like < END else ():
        for _key in (_item[0], f"{_item[0]}.{_item[1]}"):
            _count[_key] = _count.get(_key, 0) + 1
PER_LOOP = BEFORE[LOOP_FROM + 1] - BEFORE[LOOP_FROM]
assert PER_LOOP % 2 == 0


class Seen:

    def __init__(self, like, i):
        self.like, self.i, self.within = like, i, {}

    def after(self, name, part):
        for key in (name, f"{name}.{part}"):
            self.within[key] = self.within.get(key, 0) + 1

    def __call__(self, name):
        n = STARTED[self.like].get(name, 0) + self.within.get(name, 0)
        if isinstance(self.i, int):
            return n
        assert n > 0, name
        return n + (self.i - LOOP_FROM) * (STARTED[LOOP_FROM + 1][name] - STARTED[LOOP_FROM][name])


def ordered(like, i):
    seen = Seen(like, i)
    for item in items(like, i):
        yield item, seen
        seen.after(item[0], item[1])


MAX_TILES = ((3,), (2,), (1, 0))
EXP_TILES = ((0,), (1,), (2, 3))


def widths(kind):
    return [min(T, P * (q + 1) + LAST[kind]) for q in range(TB)]


def block_kernel(nc, x, ctx, logits, w_qkv, w_proj1, w_q2, w_kv2, w_proj2, w_fc, w_mlp, cols, rows, out):
    with ExitStack() as stack:
        def sb(name, shape, dt=F32):
            return stack.enter_context(nc.sbuf_tensor(name, shape, dt))

        def sem(name):
            return stack.enter_context(nc.semaphore(name))

        max_scores = stack.enter_context(nc.psum_tensor("max_scores", [P, MAX_BANKS, T], F32))
        scores = stack.enter_context(nc.psum_tensor("scores", [P, EXP_BANKS, T], F32))
        pv_out = stack.enter_context(nc.psum_tensor("pv_out", [P, T], F32))
        dense = stack.enter_context(nc.psum_tensor("dense", [P, 2, T], F32))

        qkv_w = sb("qkv_w", [P, HC, 3 * H])
        proj1_w = sb("proj1_w", [P, HC, H])
        q2_w = sb("q2_w", [P, HC, H])
        kv2_w = sb("kv2_w", [P, HC, 2 * H])
        proj2_w = sb("proj2_w", [P, HC, H])
        fc_w = sb("fc_w", [P, HC, INNER])
        mlp_w = sb("mlp_w", [P, FC, H])
        col = sb("col", [P, NCOL])
        row = sb("row", [P, len(ROWS), H])
        ident = sb("ident", [P, P])
        ident_b = sb("ident_b", [P, P], BF16)
        mask = {"self": sb("mask_self", [P, P], BF16), "cross": sb("mask_cross", [P, P + 2], BF16)}
        minus_half = sb("minus_half", [P, TB])

        x_in = sb("x_in", [P, TB, H])
        hidden1 = sb("hidden1", [P, TB, H])
        hold = sb("hold", [P, TB, H])
        hidden2 = sb("hidden2", [P, TB, H])
        normed = sb("normed", [P, TB, H])
        attn_out = sb("attn_out", [P, TB, H])
        feat_a = sb("feat_a", [P, HC, T])
        feat_b = sb("feat_b", [P, HC, T])
        inner = sb("inner", [P, FC, T])
        key_bias = inner[0:1, 0, :]
        key_rest = inner[0:1, 1:3, :]
        key_parts = inner[0:1, 3:5, :].bitcast(BF16).rearrange("p a (b t) -> p (a b) t", t=T)
        signs_both = inner[0:3, 5, :].bitcast(BF16)
        signs = {"minus": signs_both[:, 0:T], "plus": signs_both[:, T:2 * T]}
        parts = {s: sb(f"parts_{s}", [P, 3, HC, T], BF16) for s in "qk"}
        rest = {s: sb(f"rest_{s}", [P, HC, T]) for s in "qk"}
        q_stack = {k: sb(f"q_stack_{k}", [KALL[k], NH, T], BF16) for k in KALL}
        k_stack = {k: sb(f"k_stack_{k}", [KALL[k], NH, T], BF16) for k in KALL}
        v_ones = {k: sb(f"v_ones_{k}", [P, TB, VROW]) for k in KALL}
        row_max = sb("row_max", [P, 2, GH * TB])
        max_parts = sb("max_parts", [P, P], BF16)
        max_rows = sb("max_rows", [2 * GH * TB, P], BF16)
        WMAX = sum(widths("cross"))
        probs = sb("probs", [P, 2 * GH, WMAX])
        o_turn = sb("o_turn", [P, T])
        recip = sb("recip", [P, 2, TB, GH])
        stats = sb("stats", [P, TB, 6])
        mean_var = sb("mean_var", [P, TB, 2])
        var_eps = sb("var_eps", [P, TB])
        rstd = sb("rstd", [P, TB])
        mean_rstd = sb("mean_rstd", [P, TB])
        shift = sb("shift", [P, TB])

        qkv_loaded = sem("qkv_loaded")
        weights_loaded = sem("weights_loaded")
        params_loaded = sem("params_loaded")
        consts_pool = sem("consts_pool")
        consts_dve = sem("consts_dve")
        const_rows_loaded = sem("const_rows_loaded")
        bias_rows_loaded = sem("bias_rows_loaded")
        x_loaded = sem("x_loaded")
        ctx_loaded = sem("ctx_loaded")
        resid_loaded = sem("resid_loaded")
        out_stored = sem("out_stored")
        stack_loaded = {n: sem(f"{n}_stacked") for n in ("q1", "k1", "q2", "k2")}
        max_loaded = sem("max_loaded")
        dense_made = sem("dense_made")
        max_scores_made = sem("max_scores_made")
        max_scores_read = sem("max_scores_read")
        scores_made = sem("scores_made")
        exp_done = sem("exp_done")
        masked = sem("masked")
        pv_done = sem("pv_done")
        o_copied = sem("o_copied")
        max_hi = sem("max_hi")
        max_split = sem("max_split")
        max_rows_ready = sem("max_rows_ready")
        recip_ready = sem("recip_ready")
        attn_ready = sem("attn_ready")
        turned = {n: sem(f"{n}_turned") for n in ("t1", "tc", "tx", "t2", "ta1", "ta2")}
        hi = {n: sem(f"{n}_hi") for n in stack_loaded}
        remains = {n: sem(f"{n}_rest") for n in stack_loaded}
        mid = {n: sem(f"{n}_mid") for n in stack_loaded}
        lo = {n: sem(f"{n}_lo") for n in stack_loaded}
        v_ready = {n: sem(f"{n}_ready") for n in ("v1", "v2")}
        sum_ready = {n: sem(f"{n}_sum") for n in ("p1", "p2")}
        inner_ready = sem("inner_ready")
        gelu_ready = sem("gelu_ready")
        out_ready = sem("out_ready")
        resid_ready = {n: sem(f"{n}_added") for n in ("R1", "R2", "R3")}
        stats_ready = {n: sem(f"stats_{n}") for n in ("t1", "tx", "t2")}
        aggr_ready = {n: sem(f"aggr_{n}") for n in ("t1", "tx", "t2")}
        norm_step = {n: sem(f"norm_step_{n}") for n in ("t1", "tx", "t2")}
        norm_ready = {n: sem(f"norm_{n}") for n in ("t1", "tx", "t2")}

        gates_passed = sem("gates_passed")

        block = stack.enter_context(nc.Block())

        def dense_of(like, i):
            if LOOP_FROM <= like < LOOP_TO:
                return BEFORE[LOOP_FROM] + (i - LOOP_FROM) * PER_LOOP
            return BEFORE[like]

        def wait(eng, sem_, value):
            if not (isinstance(value, int) and value <= 0):
                eng.wait_ge(sem_, value)

        def gate(eng, sem_, value):
            eng.wait_ge(sem_, value)
            eng.sem_inc(gates_passed, 1)

        def iterations(eng, body):
            for like in range(FIRST, LOOP_FROM):
                body(like, like)
            with eng.Fori(LOOP_FROM, LOOP_TO) as i:
                body(LOOP_FROM, i)
            for like in range(LOOP_TO, END):
                body(like, like)

        def released(item):
            name, part, _, b, at, g = item
            if name == "MT":
                return max_rows_ready, at.n * NG + g + 1
            if name == "ON":
                return attn_ready, at.n * NG + g + 1
            if name in turned:
                return turned[name], b * HC + part + 1
            if name in remains:
                return remains[name], b * HC + part + 1
            if name in v_ready:
                return v_ready[name], b * 2 + part + 1
            if name in sum_ready:
                return sum_ready[name], b * 2 + part + 1
            if name == "f":
                return inner_ready, b * FC + part + 1
            return out_ready, b * TB + part + 1

        def mask_of(kind, q):
            return mask[kind][:, 0:widths(kind)[q] - P * q]

        def prob_cols(kind):
            at, found = 0, []
            for k in range(TB):
                w = widths(kind)[TB - 1 - k]
                found.append((at, T - w, w))
                at += w
            return found

        @block.sync
        def _(sp):
            sp.dma_start(x_in[:], x[0].rearrange("(t p) h -> p t h", p=P)).then_inc(x_loaded, 16)
            sp.dma_start(col[:], cols).then_inc(params_loaded, 16)
            sp.dma_start(qkv_w[:], w_qkv.rearrange("(c p) n -> p c n", p=P)).then_inc(qkv_loaded, 16)
            sp.dma_start(row[:], rows.partition_broadcast(P)).then_inc(params_loaded, 16)
            sp.dma_start(key_bias[:], logits).then_inc(params_loaded, 16)
            for dst, src in ((proj1_w, w_proj1), (kv2_w, w_kv2), (q2_w, w_q2), (proj2_w, w_proj2),
                             (fc_w, w_fc), (mlp_w, w_mlp)):
                sp.dma_start(dst[:], src.rearrange("(c p) n -> p c n", p=P)).then_inc(weights_loaded, 16)
            sp.wait_ge(consts_pool, POOL_CONSTS)
            for dst, src in ((k_stack["self"][KMAX["self"]:KALL["self"], :, :], signs["minus"][0:2, :]),
                             (k_stack["cross"][KMAX["cross"]:KALL["cross"], :, :], signs["minus"][0:2, :]),
                             (q_stack["cross"][STACK:KMAX["cross"], :, :], signs["plus"][:])):
                sp.dma_start(dst, src.unsqueeze(1).to_broadcast([src.shape[0], NH, T])
                             ).then_inc(const_rows_loaded, 16)
            sp.wait_ge(consts_dve, DVE_CONSTS)
            for r in range(3):
                sp.dma_start(k_stack["cross"][STACK + r:STACK + r + 1, :, :],
                             key_parts[0:1, r:r + 1, :].to_broadcast([1, NH, T])).then_inc(bias_rows_loaded, 16)

            def body(like, i):
                for (name, part, blike, b, at, g), seen in ordered(like, i):
                    if name == "dR":
                        wait(sp, resid_ready["R2"], seen("R2"))
                        sp.dma_start(hidden1[:], x[b].rearrange("(t p) h -> p t h", p=P)).then_inc(resid_loaded, 16)
                    if name == "tc" and part == HC - 1 and blike < NB - 1:
                        wait(sp, turned["tc"], (b + 1) * HC)
                        if blike + 2 < NB:
                            sp.dma_start(x_in[:], x[b + 2].rearrange("(t p) h -> p t h", p=P)).then_inc(x_loaded, 16)
                        else:
                            sp.dma_start(x_in[:], ctx[NB - 1].rearrange("(t p) h -> p t h", p=P)).then_inc(ctx_loaded, 16)
                    if name == "t1" and part == HC - 1:
                        wait(sp, turned["t1"], (b + 1) * HC)
                        if blike > 0:
                            sp.dma_start(x_in[:], ctx[b - 1].rearrange("(t p) h -> p t h", p=P)).then_inc(ctx_loaded, 16)
                        else:
                            sp.dma_start(x_in[:], x[1].rearrange("(t p) h -> p t h", p=P)).then_inc(x_loaded, 16)
                    if name in ("dq1", "dk1", "dq2", "dk2"):
                        name = name[1:]
                        kind = "self" if name[1] == "1" else "cross"
                        dst = (q_stack if name[0] == "q" else k_stack)[kind]
                        if kind == "cross":
                            sp.wait_ge(hi[name], (b + 1) * HC)
                        if blike > 0:
                            before = Attn(kind, blike - 1 + (kind == "cross"), b - 1 + (kind == "cross"))
                            wait(sp, scores_made, (before.n + 1) * BEATS)
                        src = parts[name[0]]
                        for p_, ready in ((0, hi), (1, mid), (2, lo)):
                            if ready is not hi or kind == "self":
                                sp.wait_ge(ready[name], (b + 1) * HC)
                            for r, which in enumerate(PARTS[name[0]]):
                                if which == p_:
                                    sp.dma_start(dst[r * HD:(r + 1) * HD, :, :],
                                                 src[:, p_].rearrange("p c t -> p (c t)")).then_inc(stack_loaded[name], 16)
                    if name == "MT":
                        sp.wait_ge(max_rows_ready, at.n * NG + g + 1)
                        sp.dma_start(q_stack[at.kind][KMAX[at.kind]:KALL[at.kind], g * GH:(g + 1) * GH, :],
                                     max_rows[:]).then_inc(max_loaded, 16)
                    if name == "m":
                        sp.wait_ge(out_ready, b * TB + part + 1)
                        sp.dma_start(out[b, part * P:(part + 1) * P, :], hidden2[:, part, :]).then_inc(out_stored, 16)

            iterations(sp, body)
            sp.wait_ge(out_stored, NB * TB * 16)

        @block.tensor
        def _(pe):
            pe.wait_ge(consts_pool, POOL_CONSTS)
            pe.wait_ge(qkv_loaded, 16)

            def turn(dst, src, part):
                for t in range(TB):
                    last = pe.transpose(dst[:, t * P:(t + 1) * P], src[:, t, part * P:(part + 1) * P], ident[:])
                return last

            def by_feature(dst, w, at, src):
                for c in range(HC):
                    last = pe.matmul(dst, w[:, c, at:at + P], src[:, c, :], start=(c == 0), stop=(c == HC - 1))
                return last

            def by_token(dst, src, w, at, t, some=range(HC), chunks=HC):
                for c in some:
                    last = pe.matmul(dst, src[:, c, t * P:(t + 1) * P], w[:, c, at:at + H],
                                     start=(c == 0), stop=(c == chunks - 1))
                return last

            def body(like, i):
                k = 0
                recent = [x_ for x_ in items(like - 1, i - 1) if is_dense(x_[0])] if like > FIRST else []

                def claim():
                    if len(recent) >= 2:
                        wait(pe, *released(recent[-2]))
                    return (BEFORE[like] + k) % 2

                for item in items(like, i):
                    name, part, blike, b, at, g = item
                    if name == "M":
                        head, r = part // TILES, part % TILES
                        if part == 0:
                            n = "1" if at.kind == "self" else "2"
                            pe.wait_ge(stack_loaded["q" + n], (at.b + 1) * 6 * 16)
                            pe.wait_ge(stack_loaded["k" + n], (at.b + 1) * 6 * 16)
                            if at.kind == "self" and at.like == 0:
                                pe.wait_ge(const_rows_loaded, 3 * 16)
                                pe.wait_ge(consts_dve, 1)
                            if at.kind == "cross" and at.like == 0:
                                pe.wait_ge(bias_rows_loaded, 3 * 16)
                        rows_ = KMAX[at.kind]
                        W = widths(at.kind)
                        bank = part % MAX_BANKS
                        wait(pe, max_scores_read, at.n * BEATS + part + 1 - MAX_BANKS)
                        c0 = 0
                        for q in MAX_TILES[r]:
                            pe.matmul(max_scores[:, bank, c0:c0 + W[q]],
                                      q_stack[at.kind][0:rows_, head, q * P:(q + 1) * P],
                                      k_stack[at.kind][0:rows_, head, 0:W[q]], start=True, stop=False)
                            last = pe.matmul(max_scores[:, bank, c0 + q * P:c0 + W[q]], ident_b[:],
                                             mask_of(at.kind, q), start=False, stop=True)
                            c0 += W[q]
                        last.then_inc(max_scores_made, 1)
                    elif name == "S":
                        head, r = part // TILES, part % TILES
                        if part % GT == 0:
                            pe.wait_ge(max_loaded, (at.n * NG + g + 1) * 16)
                        rows_ = KALL[at.kind]
                        wait(pe, exp_done, at.n * BEATS + part + 1 - EXP_BANKS)
                        c0 = 0
                        for kb in EXP_TILES[r]:
                            _, q0, w = prob_cols(at.kind)[kb]
                            last = pe.matmul(scores[:, part % EXP_BANKS, c0:c0 + w],
                                             k_stack[at.kind][0:rows_, head, kb * P:(kb + 1) * P],
                                             q_stack[at.kind][0:rows_, head, q0:T], start=True, stop=True)
                            c0 += w
                        last.then_inc(scores_made, 1)
                    elif name == "PV":
                        if part == 0:
                            pe.wait_ge(masked, at.n * NH * 2 + (g + 1) * GH * 2)
                            if g == 0:
                                pe.wait_ge(v_ready["v1" if at.kind == "self" else "v2"], (at.b + 1) * 2)
                        c0, q0, w = prob_cols(at.kind)[part]
                        for j in range(GH):
                            head = g * GH + j
                            last = pe.matmul(pv_out[32 * j:32 * j + 32, q0:T],
                                             v_ones[at.kind][:, part, head * VW:head * VW + 32],
                                             probs[:, head % (2 * GH), c0:c0 + w],
                                             start=(part == 0), stop=(part == TB - 1))
                        if part == TB - 1:
                            last.then_inc(pv_done, 1)
                    if name == "ma":
                        bank = claim()
                        pe.wait_ge(gelu_ready, b * 2 + 1)
                        by_token(dense[:, bank, 0:H], inner, mlp_w, 0, part, range(FC // 2), FC)
                    if not is_dense(name):
                        continue
                    bank = (BEFORE[like] + k) % 2 if name == "m" else claim()
                    recent.append(item)
                    k += 1
                    d = dense[:, bank, :]
                    if name == "MT":
                        pe.wait_ge(max_split, at.n * NG + g + 1)
                        last = pe.transpose(d.bitcast(BF16)[:, 0:P], max_parts[:], ident_b[:])
                    elif name == "ON":
                        pe.wait_ge(o_copied, at.n * NG + g + 1)
                        for t in range(TB):
                            last = pe.transpose(d[:, t * P:(t + 1) * P], o_turn[:, t * P:(t + 1) * P], ident[:])
                    elif name in ("t1", "tx", "t2"):
                        pe.wait_ge(norm_ready[name], (b + 1) * TB)
                        last = turn(d, x_in if name == "t1" else normed, part)
                    elif name == "tc":
                        pe.wait_ge(ctx_loaded, (b + 1) * 16)
                        last = turn(d, x_in, part)
                    elif name in ("ta1", "ta2"):
                        kind = "self" if name == "ta1" else "cross"
                        a = Attn(kind, blike + (kind == "cross"), b + (kind == "cross"))
                        pe.wait_ge(attn_ready, (a.n + 1) * NG)
                        last = turn(d, attn_out, part)
                    elif name in ("q1", "k1"):
                        pe.wait_ge(turned["t1"], (b + 1) * HC)
                        last = by_feature(d, qkv_w, (name == "k1") * H + part * P, feat_a)
                    elif name == "q2":
                        pe.wait_ge(turned["tx"], (b + 1) * HC)
                        last = by_feature(d, q2_w, part * P, feat_b)
                    elif name == "k2":
                        pe.wait_ge(turned["tc"], (b + 1) * HC)
                        last = by_feature(d, kv2_w, part * P, feat_a)
                    elif name in ("v1", "v2"):
                        pe.wait_ge(turned["t1" if name == "v1" else "tc"], (b + 1) * HC)
                        w, c0 = (qkv_w, 2 * H) if name == "v1" else (kv2_w, H)
                        for t in range(2):
                            last = by_token(d[:, t * H:(t + 1) * H], feat_a, w, c0, 2 * part + t)
                    elif name in ("p1", "p2"):
                        pe.wait_ge(turned["ta1" if name == "p1" else "ta2"], (b + 1) * HC)
                        for t in range(2):
                            last = by_token(d[:, t * H:(t + 1) * H], feat_b,
                                            proj1_w if name == "p1" else proj2_w, 0, 2 * part + t)
                    elif name == "f":
                        pe.wait_ge(turned["t2"], (b + 1) * HC)
                        last = by_feature(d, fc_w, part * P, feat_b)
                    else:
                        pe.wait_ge(gelu_ready, b * 2 + 2)
                        last = by_token(d[:, 0:H], inner, mlp_w, 0, part, range(FC // 2, FC), FC)
                    last.then_inc(dense_made, 1)
                if like == FIRST:
                    pe.wait_ge(weights_loaded, 6 * 16)

            iterations(pe, body)

        @block.scalar
        def _(act):
            act.wait_ge(params_loaded, 3 * 16)

            def column(name, part):
                at = COLS[name][0] + part
                return col[:, at:at + 1]

            def body(like, i):
                made = dense_of(like, i)
                for (name, part, blike, b, at, g), seen in ordered(like, i):
                    if is_dense(name):
                        made = made + 1
                        d = dense[:, (BEFORE[like] + is_first[0]) % 2, :]
                        is_first[0] += 1
                    if name == "S":
                        head, r = part // TILES, part % TILES
                        if part % GT == 0:
                            wait(act, pv_done, at.n * NG + g - 1)
                        cols_ = prob_cols(at.kind)
                        c0, w = cols_[EXP_TILES[r][0]][0], sum(cols_[kb][2] for kb in EXP_TILES[r])
                        act.wait_ge(scores_made, at.n * BEATS + part + 1)
                        nc.scalar.activation(probs[:, head % (2 * GH), c0:c0 + w], scores[:, part % EXP_BANKS, 0:w],
                                             ACT.Exp, scale=SCALE).then_inc(exp_done, 1)
                    elif name == "PV" and part == TB - 1:
                        act.wait_ge(pv_done, at.n * NG + g + 1)
                        nc.scalar.copy(o_turn[:], pv_out[:]).then_inc(o_copied, 1)
                    elif name in ("t1", "tx", "t2"):
                        ln = {"t1": "ln1", "tx": "lnx", "t2": "ln2"}[name]
                        act.wait_ge(dense_made, made)
                        nc.scalar.activation((feat_a if name == "t1" else feat_b)[:, part, :], d, ACT.Identity,
                                             bias=column(ln + "_b", part), scale=column(ln + "_g", part)
                                             ).then_inc(turned[name], 1)
                    elif name in ("tc", "ta1", "ta2"):
                        act.wait_ge(dense_made, made)
                        nc.scalar.copy((feat_a if name == "tc" else feat_b)[:, part, :], d).then_inc(turned[name], 1)
                    elif name in hi:
                        if part == 0:
                            for n in "12":
                                wait(act, stack_loaded[name[0] + n], seen("d" + name[0] + n) * 96)
                        act.wait_ge(dense_made, made)
                        nc.scalar.activation(parts[name[0]][:, 0, part, :], d, ACT.Identity,
                                             bias=column(name, part)).then_inc(hi[name], 1)
                    elif name == "f":
                        act.wait_ge(dense_made, made)
                        nc.scalar.activation(inner[:, part, :], d, ACT.Identity,
                                             bias=column("fc_b", part)).then_inc(inner_ready, 1)
                    elif name == "G":
                        act.wait_ge(inner_ready, b * FC + (part + 1) * FC // 2)
                        v = inner[:, part * FC // 2:(part + 1) * FC // 2, :]
                        nc.scalar.activation(v, v, ACT.Gelu_apprx_tanh).then_inc(gelu_ready, 1)

            is_first = [0]

            def counted(like, i):
                is_first[0] = 0
                body(like, i)

            iterations(act, counted)

        @block.vector
        def _(dve):
            for kind in KALL:
                nc.vector.memset(v_ones[kind][:], 1.0)
            nc.vector.memset(max_parts[:], 0.0)
            dve.wait_ge(consts_pool, POOL_CONSTS)
            nc.vector.tensor_copy(ident_b[:], ident[:]).then_inc(consts_dve, 1)
            dve.wait_ge(params_loaded, 3 * 16)
            steps = (
                lambda: nc.vector.tensor_scalar_mul(key_bias[:], key_bias[:], 1.0 / SCALE),
                lambda: nc.vector.tensor_copy(key_parts[:, 0, :], key_bias[:]),
                lambda: nc.vector.tensor_tensor(key_rest[:, 0, :], key_bias[:], key_parts[:, 0, :], ALU.subtract),
                lambda: nc.vector.tensor_copy(key_parts[:, 1, :], key_rest[:, 0, :]),
                lambda: nc.vector.tensor_tensor(key_rest[:, 1, :], key_rest[:, 0, :], key_parts[:, 1, :], ALU.subtract),
                lambda: nc.vector.tensor_copy(key_parts[:, 2, :], key_rest[:, 1, :]),
            )
            for n, step in enumerate(steps):
                if n:
                    dve.wait_ge(consts_dve, n + 1)
                step().then_inc(consts_dve, 1)

            def column(name, part):
                at = COLS[name][0] + part
                return col[:, at:at + 1]

            def bias_row(name):
                return row[:, ROWS.index(name), :]

            def statistics(name, src, b, seen):
                wait(dve, norm_step["t1"], seen("L1") * 4)
                wait(dve, norm_step["tx"], seen("p1.1") * 4)
                wait(dve, norm_step["t2"], seen("p2.1") * 4)
                for t in range(TB):
                    last = nc.vector.bn_stats(stats[:, t, :], src[:, t, :])
                last.then_inc(stats_ready[name], 1)
                gate(dve, stats_ready[name], b + 1)
                for t in range(TB):
                    last = nc.vector.bn_aggr(mean_var[:, t, :], stats[:, t, :])
                last.then_inc(aggr_ready[name], 1)

            def body(like, i):
                made, k = dense_of(like, i), 0
                for (name, part, blike, b, at, g), seen in ordered(like, i):
                    if is_dense(name):
                        made = made + 1
                        d = dense[:, (BEFORE[like] + k) % 2, :]
                        k += 1
                    if name == "L1":
                        dve.wait_ge(x_loaded, (b + 1) * 16)
                        statistics("t1", x_in, b, seen)
                    elif name == "M":
                        j, r = part // TILES % GH, part % TILES
                        W = widths(at.kind)
                        dve.wait_ge(max_scores_made, at.n * BEATS + part + 1)
                        c0 = 0
                        for q in MAX_TILES[r]:
                            c = j * TB + q
                            last = nc.vector.tensor_reduce(row_max[:, g % 2, c:c + 1],
                                                           max_scores[:, part % MAX_BANKS, c0:c0 + W[q]],
                                                           AX.X, ALU.max)
                            c0 += W[q]
                        last.then_inc(max_scores_read, 1)
                        if part % GT == GT - 1:
                            n = GH * TB
                            dve.wait_ge(max_scores_read, at.n * BEATS + (g + 1) * GT)
                            nc.vector.tensor_copy(max_parts[:, 0:n], row_max[:, g % 2, :]).then_inc(max_hi, 1)
                            dve.wait_ge(max_hi, at.n * NG + g + 1)
                            nc.vector.tensor_tensor(max_parts[:, n:2 * n], row_max[:, g % 2, :], max_parts[:, 0:n],
                                                    ALU.subtract).then_inc(max_split, 1)
                    elif name == "MT":
                        dve.wait_ge(dense_made, made)
                        wait(dve, max_loaded, (at.n * NG + g) * 16)
                        nc.vector.tensor_copy(max_rows[:], d.bitcast(BF16)[0:2 * GH * TB, 0:P]).then_inc(max_rows_ready, 1)
                    elif name == "ON":
                        o = d.rearrange("p (q h e) -> p q h e", q=TB, h=GH)
                        dve.wait_ge(dense_made, made)
                        nc.vector.reciprocal(recip[:, g % 2], o[:, :, :, HD]).then_inc(recip_ready, 1)
                        dve.wait_ge(recip_ready, at.n * NG + g + 1)
                        dst = attn_out[:, :, g * GH * HD:(g + 1) * GH * HD]
                        nc.vector.tensor_tensor(dst.rearrange("p q (h e) -> p q h e", h=GH), o[:, :, :, 0:HD],
                                                recip[:, g % 2].unsqueeze(3).to_broadcast([P, TB, GH, HD]),
                                                ALU.mult).then_inc(attn_ready, 1)
                    elif name in hi:
                        n = b * HC + part + 1
                        wait(dve, lo[name], b * HC)
                        wait(dve, lo[other(name)], seen(other(name)))
                        dve.wait_ge(hi[name], n)
                        nc.vector.scalar_tensor_tensor(out=rest[name[0]][:, part, :], in0=d, scalar=column(name, part),
                                                       in1=parts[name[0]][:, 0, part, :], op0=ALU.add,
                                                       op1=ALU.subtract).then_inc(remains[name], 1)
                        dve.wait_ge(remains[name], n)
                        nc.vector.tensor_copy(parts[name[0]][:, 1, part, :], rest[name[0]][:, part, :]).then_inc(mid[name], 1)
                    elif name in v_ready:
                        dve.wait_ge(dense_made, made)
                        kind = "self" if name == "v1" else "cross"
                        for t in range(2):
                            dst = v_ones[kind][:, 2 * part + t, 0:NH * VW].rearrange("p (h e) -> p h e", e=VW)[:, :, 0:HD]
                            last = nc.vector.tensor_tensor(
                                dst, d[:, t * H:(t + 1) * H].rearrange("p (h e) -> p h e", e=HD),
                                bias_row(name).rearrange("p (h e) -> p h e", e=HD), ALU.add)
                        last.then_inc(v_ready[name], 1)
                    elif name in sum_ready:
                        h = hidden1 if name == "p1" else hidden2
                        dve.wait_ge(dense_made, made)
                        if part == 0:
                            dve.wait_ge(resid_ready["R1" if name == "p1" else "R2"], b + 1)
                            if name == "p2":
                                wait(dve, out_stored, seen("m") * 16)
                        hv, rv = (v[:, 2 * part:2 * part + 2, :].rearrange("p t h -> p (t h)")
                                  for v in (h, hidden1 if name == "p1" else hold))
                        nc.vector.tensor_tensor(hv, d, rv, ALU.add).then_inc(sum_ready[name], 1)
                        if part == 1:
                            dve.wait_ge(sum_ready[name], 2 * b + 2)
                            statistics("tx" if name == "p1" else "t2", h, b, seen)
                    elif name == "m":
                        dve.wait_ge(dense_made, made)
                        if part == 0:
                            dve.wait_ge(resid_ready["R3"], b + 1)
                        nc.vector.tensor_tensor(hidden2[:, part, :], d[:, 0:H], hidden2[:, part, :],
                                                ALU.add).then_inc(out_ready, 1)

            iterations(dve, body)

        @block.gpsimd
        def _(pool):
            nc.gpsimd.memset(ident[:], 0.0).then_inc(consts_pool, 1)
            for kind in mask:
                nc.gpsimd.memset(mask[kind][:], 0.0).then_inc(consts_pool, 1)
            nc.gpsimd.memset(minus_half[:], -0.5).then_inc(consts_pool, 1)
            nc.gpsimd.memset(signs["minus"][:], -1.0).then_inc(consts_pool, 1)
            nc.gpsimd.memset(signs["plus"][:], 1.0).then_inc(consts_pool, 1)
            pool.wait_ge(consts_pool, 6)
            nc.gpsimd.affine_select(out=ident[:], in_=ident[:], compare_op=ALU.not_equal, fill=1.0, base=0,
                                    pattern=[[-1, P]], channel_multiplier=1).then_inc(consts_pool, 1)
            for kind in mask:
                nc.gpsimd.affine_select(out=mask[kind][:], in_=mask[kind][:], compare_op=ALU.is_ge, fill=NEG,
                                        base=LAST[kind], pattern=[[-1, P + LAST[kind]]],
                                        channel_multiplier=1).then_inc(consts_pool, 1)
            pool.wait_ge(consts_pool, POOL_CONSTS)
            pool.wait_ge(params_loaded, 3 * 16)

            def add_row(dst, src, name):
                return nc.gpsimd.tensor_tensor(dst, src, row[:, ROWS.index(name):ROWS.index(name) + 1, :]
                                               .to_broadcast([P, TB, H]), ALU.add)

            def normalise(name, dst, src, b):
                gate(pool, aggr_ready[name], b + 1)
                nc.gpsimd.tensor_scalar(var_eps[:], mean_var[:, :, 1], EPS, None, ALU.add).then_inc(norm_step[name], 1)
                pool.wait_ge(norm_step[name], b * 4 + 1)
                nc.gpsimd.tensor_tensor(rstd[:], var_eps[:], minus_half[:], ALU.pow).then_inc(norm_step[name], 1)
                pool.wait_ge(norm_step[name], b * 4 + 2)
                nc.gpsimd.tensor_tensor(mean_rstd[:], mean_var[:, :, 0], rstd[:], ALU.mult).then_inc(norm_step[name], 1)
                gate(pool, norm_step[name], b * 4 + 3)
                nc.gpsimd.tensor_scalar(shift[:], mean_rstd[:], -1.0, None, ALU.mult).then_inc(norm_step[name], 1)
                gate(pool, norm_step[name], b * 4 + 4)
                for t in range(TB):
                    nc.gpsimd.tensor_scalar(dst[:, t, :], src[:, t, :], rstd[:, t:t + 1], shift[:, t:t + 1],
                                            ALU.mult, ALU.add).then_inc(norm_ready[name], 1)

            def body(like, i):
                for (name, part, blike, b, at, g), seen in ordered(like, i):
                    if name == "R2":
                        pool.wait_ge(sum_ready["p1"], (b + 1) * TP)
                        wait(pool, sum_ready["p2"], seen("p2"))
                        add_row(hold[:], hidden1[:], "proj2").then_inc(resid_ready["R2"], 1)
                    elif name == "R1":
                        pool.wait_ge(resid_loaded, (b + 1) * 16)
                        add_row(hidden1[:], hidden1[:], "proj1").then_inc(resid_ready["R1"], 1)
                    elif name == "L1":
                        normalise("t1", x_in, x_in, b)
                    elif name == "p1" and part == 1:
                        wait(pool, turned["t2"], seen("t2"))
                        normalise("tx", normed, hidden1, b)
                    elif name == "p2" and part == 1:
                        wait(pool, turned["tx"], seen("tx"))
                        normalise("t2", normed, hidden2, b)
                        pool.wait_ge(norm_ready["t2"], (b + 1) * TB)
                        add_row(hidden2[:], hidden2[:], "mlp").then_inc(resid_ready["R3"], 1)
                    elif name in lo:
                        pool.wait_ge(mid[name], b * HC + part + 1)
                        nc.gpsimd.tensor_tensor(parts[name[0]][:, 2, part, :], rest[name[0]][:, part, :],
                                                parts[name[0]][:, 1, part, :], ALU.subtract).then_inc(lo[name], 1)
                    elif name == "S" and part % (2 * TILES) == 2 * TILES - 1:
                        head = part // TILES
                        gate(pool, exp_done, at.n * BEATS + part + 1)
                        s0 = (head - 1) % (2 * GH)
                        for kb, (c0, q0, _) in enumerate(prob_cols(at.kind)):
                            v = probs[:, s0:s0 + 2, c0:c0 + P]
                            nc.gpsimd.affine_select(out=v, in_=v, compare_op=ALU.is_ge, fill=0.0,
                                                    base=q0 - kb * P + LAST[at.kind], pattern=[[0, 2], [1, P]],
                                                    channel_multiplier=-1).then_inc(masked, 1)

            iterations(pool, body)


DVE_CONSTS = 7
POOL_CONSTS = 9


def kernel(x, ctx_1024, L0_xattn_scorer_logits, L0_xattn_ln1_g, L0_xattn_ln1_b, L0_xattn_c_attn_w,
           L0_xattn_c_attn_b, L0_xattn_attn_proj_w, L0_xattn_attn_proj_b, L0_xattn_lnx_g, L0_xattn_lnx_b,
           L0_xattn_q_attn_w, L0_xattn_q_attn_b, L0_xattn_x_kv_w, L0_xattn_x_kv_b, L0_xattn_x_proj_w,
           L0_xattn_x_proj_b, L0_xattn_ln2_g, L0_xattn_ln2_b, L0_xattn_fc_w, L0_xattn_fc_b,
           L0_xattn_mlp_proj_w, L0_xattn_mlp_proj_b):
    import concourse.bacc as bacc
    from concourse.bass_utils import run_bass_kernel_spmd

    def split_order(w):
        lead = w.shape[:-1]
        w = w.reshape(*lead, HP, HC, HD)
        return np.moveaxis(w, (-3, -2, -1), (-1, -3, -2)).reshape(*lead, H)

    def by_partition(v):
        return np.reshape(v, (-1, P)).T

    qkv, qkv_b = np.asarray(L0_xattn_c_attn_w), np.asarray(L0_xattn_c_attn_b)
    kv, kv_b = np.asarray(L0_xattn_x_kv_w), np.asarray(L0_xattn_x_kv_b)
    q2, q2_b = np.asarray(L0_xattn_q_attn_w), np.asarray(L0_xattn_q_attn_b)
    columns = {"ln1_g": L0_xattn_ln1_g, "ln1_b": L0_xattn_ln1_b, "lnx_g": L0_xattn_lnx_g,
               "lnx_b": L0_xattn_lnx_b, "ln2_g": L0_xattn_ln2_g, "ln2_b": L0_xattn_ln2_b,
               "q1": split_order(qkv_b[:H]), "k1": split_order(qkv_b[H:2 * H]), "q2": split_order(q2_b),
               "k2": split_order(kv_b[:H]), "fc_b": L0_xattn_fc_b}
    arrays = {
        "in_x": x, "in_ctx": ctx_1024, "in_logits": L0_xattn_scorer_logits,
        "in_w_qkv": np.concatenate([split_order(qkv[:, :H]), split_order(qkv[:, H:2 * H]), qkv[:, 2 * H:]], 1),
        "in_w_proj1": L0_xattn_attn_proj_w,
        "in_w_q2": split_order(q2),
        "in_w_kv2": np.concatenate([split_order(kv[:, :H]), kv[:, H:]], 1),
        "in_w_proj2": L0_xattn_x_proj_w, "in_w_fc": L0_xattn_fc_w, "in_w_mlp": L0_xattn_mlp_proj_w,
        "in_cols": np.concatenate([by_partition(np.asarray(columns[n])) for n in COLS], 1),
        "in_rows": np.stack([qkv_b[2 * H:], np.asarray(L0_xattn_attn_proj_b), kv_b[H:],
                             np.asarray(L0_xattn_x_proj_b), np.asarray(L0_xattn_mlp_proj_b)]),
    }
    arrays = {n: np.ascontiguousarray(a) for n, a in arrays.items()}
    nc = bacc.Bacc("TRN2", target_bir_lowering=False, num_devices=1, dynamic_dma_scratch_size=1024)
    args = [nc.dram_tensor(n, a.shape, mybir.dt.from_np(a.dtype), kind="ExternalInput").ap()
            for n, a in arrays.items()]
    args.append(nc.dram_tensor("out_y", (NB, T, H), F32, kind="ExternalOutput").ap())
    block_kernel(nc, *args)
    return run_bass_kernel_spmd(nc, [arrays], core_ids=[0]).results[0]["out_y"]
```
